# Optimizing a Trainium2 kernel written in Bass

```python
import numpy as np
import jax
import jax.numpy as jnp

def _softmax(x, axis=-1):
    return jax.nn.softmax(x, axis=axis)

def _gelu(x):
    return jax.nn.gelu(x, approximate=True)

def _silu(x):
    return jax.nn.silu(x)

def _sigmoid(x):
    return jax.nn.sigmoid(x)

def _layernorm(x, axis=-1, eps=1e-05):
    m = jnp.mean(x, axis=axis, keepdims=True)
    v = jnp.var(x, axis=axis, keepdims=True)
    return (x - m) / jnp.sqrt(v + eps)

def _scatter_add(tgt, idx, src, axis=0):
    return tgt.at[idx].add(src)

def _segment_sum(src, seg, n):
    return jax.ops.segment_sum(src, seg, n)
kernel_name = 'mk_gnn_resnorm_d2_gnn_r8_ea535e'

def setup_inputs(seed: int=0):
    np.random.seed(seed)
    _w = jnp.asarray

    def _rec_inputs():
        import jax
        import jax.numpy as jnp
        _gk = jax.random.key(seed)
        x = -0.0003713 + 1 * jax.random.normal(jax.random.fold_in(_gk, 1), (12500, 256), jnp.float32)
        _s = jax.random.randint(jax.random.fold_in(_gk, 2), (100000,), 0, 12500, jnp.int32)
        _d = jax.random.randint(jax.random.fold_in(_gk, 3), (100000,), 0, 12500, jnp.int32)
        _loop = jnp.arange(12500, dtype=jnp.int32)
        src = jnp.concatenate([_s, _d, _loop])
        dst = jnp.concatenate([_d, _s, _loop])
        _o = jnp.argsort(dst, stable=True)
        src = src[_o]
        dst = dst[_o]
        edge_attr_64 = 0.000189758 + 1.00013 * jax.random.normal(jax.random.fold_in(_gk, 12), (212500, 64), jnp.float32)
        return (x, src, dst, edge_attr_64)
    x, src, dst, edge_attr_64 = _rec_inputs()

    def _L0_gnn_setup():
        import jax, jax.numpy as jnp
        import numpy as np
        N_NODES = 6250
        key = jax.random.key(seed)
        k1, k2, k3 = jax.random.split(key, 3)
        x = jax.random.normal(k1, (N_NODES, 256), dtype=jnp.float32)
        W = jax.random.normal(k2, (256, 256), dtype=jnp.float32) * (1.0 / np.sqrt(256))
        edge_index = jax.random.randint(k3, (2, 200000), 0, N_NODES, dtype=jnp.int64)
        return {'x': x, 'W': W, 'edge_index': edge_index}
    _L0_gnn_all = _L0_gnn_setup()
    _L0_gnn_in = {k: v for k, v in _L0_gnn_all.items() if k in ('W',)}
    del _L0_gnn_all

    def _L1_gnn_setup():
        import jax, jax.numpy as jnp
        import numpy as np
        N_NODES = 6250
        N_EDGES = 100000
        NODE_IN = 256
        EDGE_OUT = 64
        GLOBAL_IN = 128
        NODE_OUT = 256
        HIDDEN = 512
        N_GRAPHS = 64
        key = jax.random.key(seed)
        ks = jax.random.split(key, 8)
        x = jax.random.normal(ks[0], (N_NODES, NODE_IN), dtype=jnp.float32)
        edge_index = jax.random.randint(ks[1], (2, N_EDGES), 0, N_NODES, dtype=jnp.int64)
        edge_attr = jax.random.normal(ks[2], (N_EDGES, EDGE_OUT), dtype=jnp.float32)
        u = jax.random.normal(ks[3], (N_GRAPHS, GLOBAL_IN), dtype=jnp.float32)
        batch = jnp.sort(jax.random.randint(ks[4], (N_NODES,), 0, N_GRAPHS, dtype=jnp.int64))
        in_dim = NODE_IN + EDGE_OUT + GLOBAL_IN
        b1s = 1.0 / np.sqrt(in_dim)
        b2s = 1.0 / np.sqrt(HIDDEN)
        W1 = jax.random.uniform(ks[5], (in_dim, HIDDEN), dtype=jnp.float32, minval=-b1s, maxval=b1s)
        b1 = jnp.zeros((HIDDEN,), dtype=jnp.float32)
        W2 = jax.random.uniform(ks[6], (HIDDEN, NODE_OUT), dtype=jnp.float32, minval=-b2s, maxval=b2s)
        b2 = jnp.zeros((NODE_OUT,), dtype=jnp.float32)
        return {'x': x, 'edge_index': edge_index, 'edge_attr': edge_attr, 'u': u, 'batch': batch, 'W1': W1, 'b1': b1, 'W2': W2, 'b2': b2}
    _L1_gnn_all = _L1_gnn_setup()
    _L1_gnn_in = {k: v for k, v in _L1_gnn_all.items() if k in ('u', 'W1', 'b1', 'W2', 'b2')}
    del _L1_gnn_all
    return {'x': x, 'src': src, 'dst': dst, 'edge_attr_64': edge_attr_64, 'L0_gnn_W': _L0_gnn_in['W'], 'L1_gnn_u': _L1_gnn_in['u'], 'L1_gnn_W1': _L1_gnn_in['W1'], 'L1_gnn_b1': _L1_gnn_in['b1'], 'L1_gnn_W2': _L1_gnn_in['W2'], 'L1_gnn_b2': _L1_gnn_in['b2']}

def reference(x, src, dst, edge_attr_64, L0_gnn_W, L1_gnn_u, L1_gnn_W1, L1_gnn_b1, L1_gnn_W2, L1_gnn_b2):
    import jax
    import jax.numpy as jnp

    def _L0_gnn_ref(x, W, edge_index):
        import jax, jax.numpy as jnp
        import numpy as np
        N_NODES = 6250
        N = x.shape[0]
        src, dst = (edge_index[0], edge_index[1])
        h = x @ W
        deg = jax.ops.segment_sum(jnp.ones_like(dst, dtype=h.dtype), dst, num_segments=N)
        deg_inv_sqrt = jnp.where(deg > 0, jax.lax.rsqrt(jnp.maximum(deg, 1)), 0.0)
        norm = deg_inv_sqrt[src] * deg_inv_sqrt[dst]
        msgs = h[src] * norm[:, None]
        out = jax.ops.segment_sum(msgs, dst, num_segments=N)
        return out

    def _L1_gnn_ref(x, edge_index, edge_attr, u, batch, W1, b1, W2, b2):
        import jax, jax.numpy as jnp
        import numpy as np
        N_NODES = 6250
        N_EDGES = 100000
        NODE_IN = 256
        EDGE_OUT = 64
        GLOBAL_IN = 128
        NODE_OUT = 256
        HIDDEN = 512
        N_GRAPHS = 64
        n = x.shape[0]
        src = edge_index[0]
        sums = jax.ops.segment_sum(edge_attr, src, num_segments=n)
        counts = jax.ops.segment_sum(jnp.ones((edge_attr.shape[0],), edge_attr.dtype), src, num_segments=n)
        edge_attr_agg = sums / jnp.maximum(counts, 1.0)[:, None]
        u_expanded = u[batch]
        combined = jnp.concatenate([x, edge_attr_agg, u_expanded], axis=1)
        h = jax.nn.relu(combined @ W1 + b1)
        return h @ W2 + b2
    edge_index = jnp.stack([src, dst])
    batch0 = jnp.zeros((12500,), jnp.int32)
    x = _layernorm(x + _L0_gnn_ref(x, L0_gnn_W, edge_index), axis=-1)
    x = _layernorm(x + _L1_gnn_ref(x, edge_index, edge_attr_64, L1_gnn_u, batch0, L1_gnn_W1, L1_gnn_b1, L1_gnn_W2, L1_gnn_b2), axis=-1)
    return x

_drawn_inputs = setup_inputs


def setup_inputs(seed=0):
    import zlib

    import numpy as np

    out = dict(_drawn_inputs(seed))
    spreads = {'L1_gnn_b1': (0.0, 0.1), 'L1_gnn_b2': (0.0, 0.1)}
    factors = {}
    for name, (base, spread) in spreads.items():
        noise = np.random.default_rng([zlib.crc32(name.encode()), seed]).standard_normal(out[name].shape)
        drawn = base * np.exp(spread * noise) if base else spread * noise
        out[name] = jnp.asarray(drawn.astype(out[name].dtype))
    for name, factor in factors.items():
        out[name] = (out[name] * factor).astype(out[name].dtype)
    return out
```

```python
import concourse.bass as bass
from concourse import mybir
from contextlib import ExitStack

F32 = mybir.dt.float32
BF16 = mybir.dt.bfloat16
I32 = mybir.dt.int32
ALU = mybir.AluOpType
ACT = mybir.ActivationFunctionType
AX = mybir.AxisListType

P = 128
G = 4
GE = P * G
TABLES = 4
WIN = 64
WIDE = 512
NT = 125
LAG = 5
EPS = 1e-5


def gnn_kernel(nc, x, src, dst, edge_attr, W, u, W1, b1, W2, b2, out):
    N, D = x.shape
    E, DE = edge_attr.shape
    H = W1.shape[1]
    DG = u.shape[1]
    KC = D // P
    HC = H // P
    FULL = E // GE
    TAIL = E - FULL * GE
    NG = FULL + 1
    ITER = NG // G
    TILES = N // NT
    HI = (N + P - 1) // P
    ROW = DE + 1
    SPAN = (N + WIDE - 1) // WIDE * WIDE
    WINDOWS = SPAN // WIDE
    EROWS = (N + P + P - 1) // P * P
    HALF = ITER // 2
    XS = 2
    assert NG % G == 0 and 0 < TAIL <= P and TILES * NT == N and ITER % 2 == 0
    assert D == KC * P and H == HC * P and DG == P and SPAN >= N + WIN
    assert HALF + TILES // XS <= ITER - 2 and TILES >= ITER - 1 - LAG

    etab = [nc.dram_tensor(f"edge_table{k}", (EROWS, ROW), F32, kind="Internal").ap() for k in range(TABLES)]
    xs_dram = nc.dram_tensor("x_scaled", (N, D), F32, kind="Internal").ap()
    dis_dram = nc.dram_tensor("dis", (HI * P,), F32, kind="Internal").ap()

    with ExitStack() as ctx:
        def sb(name, shape, dt=F32):
            return ctx.enter_context(nc.sbuf_tensor(name, shape, dt))

        def sem(name):
            return ctx.enter_context(nc.semaphore(name))

        aggT = sb("aggT", [P, KC, SPAN])
        src_all = sb("src_all", [P, NG, G], I32)
        dst_all = sb("dst_all", [P, NG, G], I32)
        rel = sb("rel", [P, NG, G])
        hi_all = sb("hi_all", [P, NG, G], I32)
        lo_all = sb("lo_all", [P, NG, G], I32)
        base_f = sb("base_f", [1, NG])
        base_i = sb("base_i", [1, NG], I32)
        due = sb("due", [P, NG])
        late = sb("late", [P, NG])
        worst = sb("worst", [P, 4])
        flag_f = sb("flag_f", [1, 1])
        flag = sb("flag", [1, 1], I32)

        ident = sb("ident", [P, P])
        lower = sb("lower", [P, P])
        iota_col = sb("iota_col", [P, P], BF16)
        iota_win = sb("iota_win", [P, WIDE])
        ones = sb("ones", [P, P])
        ones_b = sb("ones_b", [P, 1], BF16)
        junk = sb("junk", [P, 1])
        eps = sb("eps", [P, 1])

        srcs = sb("srcs", [P, 4, G])
        rows = sb("rows", [P, 4, G, D])
        oh_wide = sb("oh_wide", [P, G, WIDE])

        def share(whole, offset, shape, dt=F32):
            free = 1
            for k in shape[1:]:
                free *= k
            words = free * mybir.dt.size(dt) // 4
            view = whole[0:shape[0]].rearrange("p a b -> p (a b)")[:, offset:offset + words]
            if dt != F32:
                view = view.bitcast(dt)
            if len(shape) == 3:
                view = view.rearrange("p (a b) -> p a b", b=shape[2])
            if len(shape) == 4:
                view = view.rearrange("p (a b c) -> p a b c", b=shape[2], c=shape[3])
            return view, offset + words

        rows_2d = rows[:].rearrange("p s g d -> p (s g) d")
        attr, used = share(rows_2d, 0, [P, 4, G, DE])
        same, used = share(rows_2d, used, [P, 2, G, P])
        stage, used = share(rows_2d, used, [P, 4, G, ROW])
        xs_in, used = share(rows_2d, used, [NT, XS, D])
        earlier, used = share(oh_wide, 0, [P, 2, G, P], BF16)
        oh_hi, used = share(oh_wide, used, [P, 2, G, HI], BF16)
        oh_lo, used = share(oh_wide, used, [P, 2, G, P], BF16)
        xs_out, used = share(oh_wide, used, [NT, XS, D])
        rep = sb("rep", [P, 2, G])
        eidx = sb("eidx", [P, 4, G], I32)
        deg = sb("deg", [HI, P])
        dmask = sb("dmask", [HI, P])
        dsq = sb("dsq", [HI, P])
        dinv = sb("dinv", [HI, P])
        dis_h = sb("dis_h", [HI, P])
        dis_t = sb("dis_t", [TILES, NT])
        dis = sb("dis_nodes", [NT, TILES])
        gidx = sb("gidx", [P, 4, G], I32)
        oh = sb("oh", [P, 2, G, WIN])
        dst_f = sb("dst_f", [P, G])
        W_sb = sb("W_sb", [P, KC, D])
        W1_sb = sb("W1_sb", [P, KC, H])
        W1e_sb = sb("W1e_sb", [DE, H])
        W1u_sb = sb("W1u_sb", [DG, H])
        W2_sb = sb("W2_sb", [P, HC, D])
        b1_sb = sb("b1_sb", [P, HC])
        b2_sb = sb("b2_sb", [NT, D])
        u_sb = sb("u_sb", [DG, 1])
        hbias = sb("hbias", [P, HC])
        aggw = sb("aggw", [P, KC, NT])
        xt = sb("xt", [NT, D])
        et = sb("et", [NT, TABLES, ROW])
        esum = sb("esum", [NT, ROW])
        ecnt = sb("ecnt", [NT, 2])
        emean = sb("emean", [NT, DE])
        r = sb("r", [NT, D])
        y = sb("y", [NT, D])
        yb = sb("yb", [NT, D])
        z = sb("z", [NT, D])
        o_sb = sb("o_sb", [NT, D])
        carrier = sb("carrier", [1, 1])
        st1 = sb("st1", [NT, 6])
        mv1 = sb("mv1", [NT, 2])
        sd1 = sb("sd1", [NT, 2])
        st2 = sb("st2", [NT, 6])
        mv2 = sb("mv2", [NT, 2])
        sd2 = sb("sd2", [NT, 2])
        yT = sb("yT", [P, KC, NT])
        eT = sb("eT", [DE, NT])
        hT = sb("hT", [P, HC, NT])

        bank = [ctx.enter_context(nc.psum_tensor(f"bank{k}", [P, 512], F32)) for k in range(8)]
        src_ps = bank[0:2]
        sum_ps = bank[2:4]
        deg_ps = bank[4]
        agg_ps = bank[5:7]
        setup_ps = bank[7]
        l0_ps, tr_ps, h_ps, o_ps = bank[2], bank[3], bank[4], bank[7]
        rep_ps = agg_ps

        src_head, src_rest, dst_in, weights_in = sem("src_head"), sem("src_rest"), sem("dst_in"), sem("weights_in")
        attr_in = [sem(f"attr_in{s}") for s in range(4)]
        xs_loaded, xs_stored, dis_stored, dis_loaded = sem("xs_loaded"), sem("xs_stored"), sem("dis_stored"), sem("dis_loaded")
        tables_zero, scattered = sem("tables_zero"), [sem(f"scattered{k}") for k in range(TABLES)]
        gathered = [sem(f"gathered{s}") for s in range(4)]
        x_loaded, e_loaded, out_stored = sem("x_loaded"), sem("e_loaded"), sem("out_stored")
        consts, pool_consts, zeroed, dst_padded = sem("consts"), sem("pool_consts"), sem("zeroed"), sem("dst_padded")
        split, based, base_bc, rel_done, check_step, worst_T, flag_ready = (
            sem("split"), sem("based"), sem("base_bc"), sem("rel_done"), sem("check_step"), sem("worst_T"), sem("flag_ready"))
        bias_mm, bias_done = sem("bias_mm"), sem("bias_done")
        src_copied, src_spread, same_done, earlier_done, summed, rep_done, idx_done, staged = (
            sem("src_copied"), sem("src_spread"), sem("same_done"), sem("earlier_done"), sem("summed"), sem("rep_done"),
            sem("idx_done"), sem("staged"))
        deg_oh, deg_mm = sem("deg_oh"), sem("deg_mm")
        deg_step, deg_root, dis_turned, dis_ready, xs_scaled = (
            sem("deg_step"), sem("deg_root"), sem("dis_turned"), sem("dis_ready"), sem("xs_scaled"))
        gidx_ready, oh_ready, agg_mm, agg_added = sem("gidx_ready"), sem("oh_ready"), sem("agg_mm"), sem("agg_added")
        wide_oh, wide_mm, wide_add, dst_copied, base_moved = (
            sem("wide_oh"), sem("wide_mm"), sem("wide_add"), sem("dst_copied"), sem("base_moved"))
        aggw_ready, l0_mm, r_done, stats1, var1, std1, rstd1, y_done, yb_done = (
            sem("aggw_ready"), sem("l0_mm"), sem("r_done"), sem("stats1"), sem("var1"), sem("std1"), sem("rstd1"),
            sem("y_done"), sem("yb_done"))
        esum_done, ecnt_done, ercp_done, emean_done = sem("esum_done"), sem("ecnt_done"), sem("ercp_done"), sem("emean_done")
        turned, turned_out, h_mm, h_relu, o_mm = sem("turned"), sem("turned_out"), sem("h_mm"), sem("h_relu"), sem("o_mm")
        z_done, stats2, var2, std2, rstd2, o_done = (
            sem("z_done"), sem("stats2"), sem("var2"), sem("std2"), sem("rstd2"), sem("o_done"))

        def at_least(eng, s, count):
            if not (isinstance(count, int) and count <= 0):
                eng.wait_ge(s, count)

        def passes(eng, last, body, first=0):
            body(first)
            if last > first + 1:
                with eng.Fori(first + 1, last) as i:
                    body(i)

        def shape_of(n):
            return (TAIL, 1) if isinstance(n, int) and n == FULL else (P, G)

        def edge_rows(a, n):
            if isinstance(n, int) and n == FULL:
                return a[FULL * GE:E, :].rearrange("(p g) f -> p g f", g=1)
            return a[bass.ds(n * GE, GE), :].rearrange("(p g) f -> p g f", g=G)

        def edge_pass(eng, step, start, count, drain):
            def iteration(i, kind):
                for s in range(G):
                    step(4 * i + s, i, s, kind)
            iteration(0, "deg")
            with eng.Fori(1, HALF - 1) as i:
                iteration(i, "deg")
            iteration(HALF - 1, "deg")
            start()
            with eng.Fori(HALF, HALF + TILES // XS) as i:
                iteration(i, "xs")
                count(i - HALF)
            for i in range(HALF + TILES // XS, ITER):
                iteration(i, "rest")
            drain()

        def nothing(*_):
            return None

        def node_pass(eng, step, dense, drain, ready=nothing):
            def iteration(i, t):
                for s in range(G):
                    step(4 * i + s, i, s)
                    if t is not None:
                        dense(t, s, 4 * i)
            iteration(0, None)
            with eng.Fori(1, LAG) as i:
                iteration(i, None)
            iteration(LAG, 0)
            with eng.Fori(LAG + 1, ITER - 1) as i:
                iteration(i, i - LAG)
            iteration(ITER - 1, ITER - 1 - LAG)
            drain()
            for t in range(ITER - LAG, TILES):
                for s in range(G):
                    dense(t, s, NG)

        def general_pass(eng, group, dense, finish=nothing):
            group(0)
            with eng.Fori(1, FULL) as n:
                group(n)
            group(FULL)
            finish()
            for s in range(G):
                dense(0, s, None)
            with eng.Fori(1, TILES - 1) as t:
                for s in range(G):
                    dense(t, s, None)
            for s in range(G):
                dense(TILES - 1, s, None)

        def by_flag(eng, fast, general):
            eng.wait_ge(flag_ready, 1)
            ok = eng.value_load(flag[0:1, 0:1], min_val=0, max_val=1)
            with eng.If(ok == 1):
                fast()
            with eng.Else():
                general()

        block = ctx.enter_context(nc.Block())

        @block.sync
        def _(sp):
            head = 16
            whole = src[0:FULL * GE].rearrange("(n p g) -> p n g", p=P, g=G)
            whole_d = dst[0:FULL * GE].rearrange("(n p g) -> p n g", p=P, g=G)
            with nc.allow_non_contiguous_dma(reason="small loads"):
                sp.dma_start(src_all[:, 0:head, :], whole[:, 0:head, :]).then_inc(src_head, 16)
                sp.wait_ge(dst_padded, 1)
                sp.dma_start(dst_all[:, 0:FULL, :], whole_d).then_inc(dst_in, 16)
                sp.dma_start(dst_all[0:TAIL, FULL, 0:1], dst[FULL * GE:E].rearrange("(p g) -> p g", g=1)).then_inc(dst_in, 16)
                sp.dma_start(src_all[:, head:FULL, :], whole[:, head:FULL, :]).then_inc(src_rest, 16)
                sp.dma_start(src_all[0:TAIL, FULL, 0:1], src[FULL * GE:E].rearrange("(p g) -> p g", g=1)).then_inc(src_rest, 16)
                sp.wait_ge(zeroed, 1)
                for k in range(TABLES):
                    sp.dma_start(etab[k].rearrange("(p r) f -> p (r f)", p=P),
                                 aggT[:].rearrange("p c n -> p (c n)")[:, 0:EROWS // P * ROW]).then_inc(tables_zero, 16)
                sp.dma_start(W_sb[:], W.rearrange("(c p) n -> p c n", p=P)).then_inc(weights_in, 16)
                sp.dma_start(W1_sb[:], W1[0:D, :].rearrange("(c p) n -> p c n", p=P)).then_inc(weights_in, 16)
                sp.dma_start(W1e_sb[:], W1[D:D + DE, :]).then_inc(weights_in, 16)
                sp.dma_start(W1u_sb[:], W1[D + DE:D + DE + DG, :]).then_inc(weights_in, 16)
                sp.dma_start(W2_sb[:], W2.rearrange("(c p) n -> p c n", p=P)).then_inc(weights_in, 16)
                sp.dma_start(b1_sb[:], b1.rearrange("(c p) -> p c", p=P)).then_inc(weights_in, 16)
                sp.dma_start(u_sb[:], u[0:1, :].rearrange("a d -> d a")).then_inc(weights_in, 16)
                sp.dma_start(b2_sb[:], b2.rearrange("(a d) -> a d", a=1).partition_broadcast(NT)).then_inc(weights_in, 16)

            def attr_load(n, i, s, kind):
                p, g = shape_of(n)
                at_least(sp, summed, n - 3)
                sp.dma_start(attr[0:p, s, 0:g, :], edge_rows(edge_attr, n)).then_inc(attr_in[s], 16)

            def dis_round_trip():
                sp.wait_ge(deg_step, 4)
                sp.dma_start(dis_dram.rearrange("(h l) -> h l", l=P), dis_h[:]).then_inc(dis_stored, 16)
                sp.wait_ge(dis_stored, 16)
                sp.dma_start(dis_t[:], dis_dram[0:N].rearrange("(t p) -> t p", p=NT)).then_inc(dis_loaded, 16)

            def xs_tiles(c):
                view = x[bass.ds(c * (XS * NT), XS * NT), :].rearrange("(k p) d -> p k d", p=NT)
                to = xs_dram[bass.ds(c * (XS * NT), XS * NT), :].rearrange("(k p) d -> p k d", p=NT)
                sp.dma_start(xs_in[:], view).then_inc(xs_loaded, 16)
                sp.wait_ge(xs_scaled, c + 1)
                sp.dma_start(to, xs_out[:]).then_inc(xs_stored, 16)

            edge_pass(sp, attr_load, dis_round_trip, xs_tiles, nothing)

            for k in range(TABLES):
                sp.wait_ge(scattered[k], 16 * (NG if k == 0 else FULL))

            def load_nodes(t):
                at_least(sp, r_done, t)
                sp.dma_start(xt[:], x[bass.ds(t * NT, NT), :]).then_inc(x_loaded, 16)
                at_least(sp, esum_done, t)
                for k in range(TABLES):
                    sp.dma_start(et[:, k, :], etab[k][bass.ds(t * NT, NT), :]).then_inc(e_loaded, 16)

            def store_nodes(t):
                sp.wait_ge(o_done, t + 1)
                sp.dma_start(out[bass.ds(t * NT, NT), :], o_sb[:]).then_inc(out_stored, 16)

            load_nodes(0)
            with sp.Fori(1, TILES) as t:
                load_nodes(t)
                store_nodes(t - 1)
            store_nodes(TILES - 1)
            sp.wait_ge(out_stored, 16 * TILES)

        @block.gpsimd
        def _(pool):
            nc.gpsimd.memset(ones[:], 1.0).then_inc(pool_consts, 1)
            nc.gpsimd.iota(iota_col[:], pattern=[[1, P]], base=0, channel_multiplier=0,
                           allow_small_or_imprecise_dtypes=True).then_inc(pool_consts, 1)
            nc.gpsimd.iota(iota_win[:], pattern=[[1, WIDE]], base=0, channel_multiplier=0,
                           allow_small_or_imprecise_dtypes=True).then_inc(pool_consts, 1)
            nc.gpsimd.iota(junk[:], pattern=[[1, 1]], base=N, channel_multiplier=1,
                           allow_small_or_imprecise_dtypes=True).then_inc(pool_consts, 1)
            nc.gpsimd.iota(due[:], pattern=[[NT, ITER], [0, G]], base=-NT * (LAG - 1), channel_multiplier=0,
                           allow_small_or_imprecise_dtypes=True).then_inc(pool_consts, 1)
            pool.wait_ge(pool_consts, 5)
            nc.gpsimd.affine_select(out=ident[:], in_=ones[:], compare_op=ALU.is_equal, fill=0.0, base=0,
                                    pattern=[[-1, P]], channel_multiplier=1).then_inc(pool_consts, 1)
            nc.gpsimd.affine_select(out=lower[:], in_=ones[:], compare_op=ALU.is_gt, fill=0.0, base=0,
                                    pattern=[[1, P]], channel_multiplier=-1).then_inc(pool_consts, 1)

            last_row, last_node = pool.to_reg(EROWS - 1), pool.to_reg(N - 1)

            def scatter(n, i, s, kind):
                p, tiles = shape_of(n)
                landed = pool.to_reg(16 * n) if not isinstance(n, int) else 16 * n
                filled = n + 1 if isinstance(n, int) else pool.to_reg(n + 1)
                pool.wait_ge(tables_zero, 16 * TABLES)
                pool.wait_ge(staged, filled)
                pool.wait_ge(idx_done, filled)
                for g in range(tiles):
                    pool.wait_ge(tables_zero, 16 * TABLES)
                    at_least(pool, scattered[g], landed)
                    pool.indirect_dma_start(
                        etab[g][:, :], bass.IndirectOffsetOnAxis(eidx[0:p, s, g:g + 1], 0),
                        stage[0:p, s, g, :], None, bounds_check=last_row, oob_is_err=True,
                        compute_op=ALU.add).then_inc(scattered[g], 16)

            edge_pass(pool, scatter, nothing, nothing, nothing)

            pool.wait_ge(summed, NG)
            for k in range(TABLES):
                pool.wait_ge(scattered[k], 16 * (NG if k == 0 else FULL))

            def gather(n, s):
                p, tiles = shape_of(n)
                copied = pool.to_reg(n + 1) if not isinstance(n, int) else n + 1
                pool.wait_ge(xs_stored, 16 * (TILES // XS))
                pool.wait_ge(gidx_ready, copied)
                for g in range(tiles):
                    pool.indirect_dma_start(
                        rows[0:p, s, g, :], None, xs_dram[:, :],
                        bass.IndirectOffsetOnAxis(gidx[0:p, s, g:g + 1], 0),
                        bounds_check=last_node, oob_is_err=True).then_inc(gathered[s], 16)

            def fast_gather(n, i, s):
                at_least(pool, agg_mm, n - 3)
                gather(n, s)

            def general_gather(n):
                at_least(pool, wide_mm, n * WINDOWS)
                gather(n, 0)

            by_flag(pool,
                    lambda: node_pass(pool, fast_gather, nothing, nothing),
                    lambda: general_pass(pool, general_gather, nothing))

        @block.scalar
        def _(act):
            act.wait_ge(src_head, 16)
            act.wait_ge(consts, 2)

            def copy_src(n, s):
                p, g = shape_of(n)
                at_least(act, idx_done, n - 3)
                nc.scalar.copy(srcs[0:p, s, 0:g], src_all[0:p, n, 0:g]).then_inc(src_copied, 1)

            def evacuate(n, i, s):
                p, g = shape_of(n)
                act.wait_ge(summed, n + 1)
                for k in range(g):
                    at_least(act, scattered[k], 16 * (n - 3))
                nc.scalar.copy(stage[0:p, s, 0:g, :].rearrange("p g f -> p (g f)"),
                               sum_ps[s % 2][0:p, 0:g * ROW]).then_inc(staged, 1)

            def edge_step(n, i, s, kind):
                if not isinstance(n, int) or n + 2 < NG:
                    if isinstance(n, int) and n == 2:
                        act.wait_ge(src_rest, 32)
                    copy_src(n + 2, (s + 2) % 4)
                if not isinstance(n, int) or n > 0:
                    evacuate(n - 1, i, (s - 1) % 4)
                if kind == "xs" and s % 2 == 1:
                    scale_tile(i - HALF, s // 2)

            def scale_tile(c, k):
                if k == 0:
                    act.wait_ge(xs_loaded, 16 * (c + 1))
                    at_least(act, xs_stored, 16 * c)
                last = nc.scalar.activation(xs_out[:, k, :], xs_in[:, k, :], ACT.Copy,
                                            scale=dis[:, bass.ds(c * XS + k, 1)])
                if k == XS - 1:
                    last.then_inc(xs_scaled, 1)

            def roots():
                act.wait_ge(deg_step, 1)
                nc.scalar.activation(dsq[:], deg[:], ACT.Sqrt).then_inc(deg_root, 1)
                act.wait_ge(dis_ready, 1)

            copy_src(0, 0)
            copy_src(1, 1)
            edge_pass(act, edge_step, roots, nothing, lambda: evacuate(NG - 1, None, (NG - 1) % 4))

            def copy_idx(n, s, first=False):
                p, g = shape_of(n)
                nc.scalar.copy(gidx[0:p, s, 0:g], src_all[0:p, n, 0:g]).then_inc(gidx_ready, 1)

            def fast_step(n, i, s):
                m, sm = n + 2, (s + 2) % 4
                if isinstance(m, int) and m >= NG:
                    return
                im = i if s < 2 else i + 1
                at_least(act, gathered[sm], 16 * G * im)
                copy_idx(m, sm)

            def dense(t, s, adds):
                if s == 0:
                    if adds is not None:
                        at_least(act, agg_added, adds)
                    at_least(act, l0_mm, t)
                    nc.scalar.copy(aggw[:], aggT[:, :, bass.ds(t * NT, NT)]).then_inc(aggw_ready, 1)
                if s == 1:
                    act.wait_ge(var1, t + 1)
                    nc.scalar.activation(sd1[:, 0:1], mv1[:, 1:2], ACT.Sqrt, bias=eps[0:NT, :]).then_inc(std1, 1)
                if s == 2:
                    act.wait_ge(turned, t + 1)
                    nc.scalar.copy(yT[:].rearrange("p c n -> p (c n)"), tr_ps[:, 0:KC * NT]).then_inc(turned_out, 1)
                    nc.scalar.copy(eT[:], tr_ps[0:DE, KC * NT:(KC + 1) * NT]).then_inc(turned_out, 1)
                    act.wait_ge(h_mm, t + 1)
                    at_least(act, o_mm, t)
                    for j in range(HC):
                        last = nc.scalar.activation(hT[:, j, :], h_ps[:, j * NT:(j + 1) * NT], ACT.Relu,
                                                    bias=hbias[:, j:j + 1])
                    last.then_inc(h_relu, 1)
                if s == 3:
                    act.wait_ge(var2, t + 1)
                    nc.scalar.activation(sd2[:, 0:1], mv2[:, 1:2], ACT.Sqrt, bias=eps[0:NT, :]).then_inc(std2, 1)

            def general_group(n):
                at_least(act, wide_mm, n * WINDOWS)
                copy_idx(n, 0)

            def fast():
                copy_idx(0, 0)
                copy_idx(1, 1)
                node_pass(act, fast_step, dense, nothing)

            act.wait_ge(bias_done, 1)
            by_flag(act, fast, lambda: general_pass(act, general_group, dense,
                                                     lambda: act.wait_ge(wide_add, NG * WINDOWS)))

        @block.vector
        def _(dve):
            V = nc.vector
            V.memset(dst_all[:, FULL, :], -1).then_inc(dst_padded, 1)
            V.memset(aggT[:], 0.0).then_inc(zeroed, 1)
            V.memset(ones_b[:], 1.0).then_inc(consts, 1)
            V.memset(eps[:], EPS).then_inc(consts, 1)
            dve.wait_ge(dst_in, 32)
            dve.wait_ge(pool_consts, 7)
            V.tensor_scalar(hi_all[:], dst_all[:], 7, None, ALU.arith_shift_right).then_inc(split, 1)
            V.tensor_scalar(lo_all[:], dst_all[:], P - 1, None, ALU.bitwise_and).then_inc(split, 1)
            V.tensor_copy(base_f[:], dst_all[0:1, :, 0]).then_inc(based, 1)
            V.tensor_copy(base_i[:], dst_all[0:1, :, 0]).then_inc(based, 1)
            dve.wait_ge(base_bc, 1)
            V.tensor_tensor(rel[:], dst_all[:], setup_ps[:, 0:NG].unsqueeze(2).to_broadcast([P, NG, G]),
                            ALU.subtract).then_inc(rel_done, 1)
            V.tensor_tensor(late[:], due[:], setup_ps[:, 0:NG], ALU.subtract).then_inc(check_step, 1)
            q = oh_wide[:].rearrange("p g w -> p (g w)")[:, 0:NG * G].rearrange("p (n g) -> p n g", g=G)
            V.memset(q[:, FULL, :], -1.0).then_inc(check_step, 1)
            dve.wait_ge(rel_done, 1)
            dve.wait_ge(check_step, 2)
            V.scalar_tensor_tensor(q[:, 0:FULL, :], rel[:, 0:FULL, :], float(1 - WIN), rel[:, 0:FULL, :],
                                   ALU.add, ALU.mult).then_inc(check_step, 1)
            V.scalar_tensor_tensor(q[0:TAIL, FULL, 0:1], rel[0:TAIL, FULL, 0:1], float(1 - WIN),
                                   rel[0:TAIL, FULL, 0:1], ALU.add, ALU.mult).then_inc(check_step, 1)
            dve.wait_ge(check_step, 4)
            V.tensor_reduce(worst[:, 0:1], q, AX.XY, ALU.max).then_inc(check_step, 1)
            V.tensor_reduce(worst[:, 1:2], late[:], AX.X, ALU.max).then_inc(check_step, 1)
            dve.wait_ge(check_step, 6)
            V.tensor_tensor(worst[:, 2:3], worst[:, 0:1], worst[:, 1:2], ALU.max).then_inc(check_step, 1)
            dve.wait_ge(worst_T, 1)
            V.tensor_reduce(flag_f[:], setup_ps[0:1, 0:P], AX.X, ALU.max).then_inc(check_step, 1)
            dve.wait_ge(check_step, 8)
            V.tensor_scalar(flag[:], flag_f[:], 0.0, None, ALU.is_le).then_inc(flag_ready, 1)

            def compare(n, i, s):
                p, g = shape_of(n)
                dve.wait_ge(src_spread, n + 1)
                at_least(dve, summed, n - 1)
                b = s % 2
                V.tensor_tensor(same[0:p, b, 0:g, 0:p],
                                src_ps[b][0:p, :].rearrange("p (g e) -> p g e", g=G)[:, 0:g, 0:p],
                                srcs[0:p, s, 0:g].unsqueeze(2).to_broadcast([p, g, p]),
                                ALU.is_equal).then_inc(same_done, 1)
                dve.wait_ge(same_done, n + 1)
                V.tensor_tensor(earlier[0:p, b, 0:g, 0:p], same[0:p, b, 0:g, 0:p],
                                lower[0:p, 0:p].unsqueeze(1).to_broadcast([p, g, p]),
                                ALU.mult).then_inc(earlier_done, 1)

            def index(n, i, s):
                p, g = shape_of(n)
                dve.wait_ge(summed, n + 1)
                V.tensor_scalar(rep[0:p, s % 2, 0:g], rep_ps[s % 2][0:p, 0:g], float(2 * EROWS),
                                junk[0:p, :], ALU.mult, ALU.min).then_inc(rep_done, 1)
                for k in range(g):
                    at_least(dve, scattered[k], 16 * (n - 3))
                dve.wait_ge(rep_done, n + 1)
                V.tensor_tensor(eidx[0:p, s, 0:g], rep[0:p, s % 2, 0:g], srcs[0:p, s, 0:g],
                                ALU.max).then_inc(idx_done, 1)

            def deg_one_hot(m, b):
                at_least(dve, deg_mm, m - 1)
                for g in range(G):
                    V.tensor_scalar(oh_hi[:, b, g, :], iota_col[:, 0:HI], hi_all[:, m, g:g + 1], None, ALU.is_equal)
                    last = V.tensor_scalar(oh_lo[:, b, g, :], iota_col[:], lo_all[:, m, g:g + 1], None, ALU.is_equal)
                last.then_inc(deg_oh, 1)

            def edge_step(n, i, s, kind):
                compare(n, i, s)
                if kind == "deg":
                    deg_one_hot(2 * n, 0)
                if not isinstance(n, int) or n > 0:
                    index(n - 1, i, (s - 1) % 4)
                if kind == "deg":
                    deg_one_hot(2 * n + 1, 1)

            def degree_factors():
                dve.wait_ge(deg_mm, NG)
                V.tensor_scalar(deg[:], deg_ps[0:HI, 0:P], 1.0, None, ALU.max).then_inc(deg_step, 1)
                V.tensor_scalar(dmask[:], deg_ps[0:HI, 0:P], 0.0, None, ALU.is_gt).then_inc(deg_step, 1)
                dve.wait_ge(deg_root, 1)
                V.reciprocal(dinv[:], dsq[:]).then_inc(deg_step, 1)
                dve.wait_ge(deg_step, 3)
                V.tensor_tensor(dis_h[:], dinv[:], dmask[:], ALU.mult).then_inc(deg_step, 1)
                dve.wait_ge(dis_turned, 1)
                V.tensor_copy(dis[:], setup_ps[0:NT, 256:256 + TILES]).then_inc(dis_ready, 1)

            dve.wait_ge(split, 2)
            edge_pass(dve, edge_step, degree_factors, nothing, lambda: index(NG - 1, None, (NG - 1) % 4))

            dve.wait_ge(bias_mm, 1)
            V.tensor_tensor(hbias[:], setup_ps[:, 400:400 + HC], b1_sb[:], ALU.add).then_inc(bias_done, 1)

            def one_hot(n, b):
                p, g = shape_of(n)
                at_least(dve, agg_mm, n - 1)
                V.tensor_tensor(oh[0:p, b, 0:g, :], rel[0:p, n, 0:g].unsqueeze(2).to_broadcast([p, g, WIN]),
                                iota_win[0:p, 0:WIN].unsqueeze(1).to_broadcast([p, g, WIN]),
                                ALU.is_equal).then_inc(oh_ready, 1)

            def add_window(n, b):
                base = dve.value_load(base_i[0:1, bass.ds(n, 1)], min_val=0, max_val=N - 1)
                dve.wait_ge(agg_mm, n + 1)
                at_least(dve, agg_added, n)
                to = aggT[:, :, bass.ds(base, WIN)]
                V.tensor_tensor(to, to, agg_ps[b][:, 0:KC * WIN].rearrange("p (c w) -> p c w", c=KC),
                                ALU.add).then_inc(agg_added, 1)

            def fast_step(n, i, s):
                one_hot(n, s % 2)
                if not isinstance(n, int) or n > 0:
                    add_window(n - 1, (s + 1) % 2)

            def dense(t, s, adds):
                if s == 0:
                    dve.wait_ge(e_loaded, 16 * TABLES * (t + 1))
                    V.tensor_reduce(esum[:], et[:].rearrange("p k f -> p f k"), AX.X, ALU.add).then_inc(esum_done, 1)
                    dve.wait_ge(esum_done, t + 1)
                    V.tensor_scalar(ecnt[:, 0:1], esum[:, DE:ROW], 1.0, None, ALU.max).then_inc(ecnt_done, 1)
                    dve.wait_ge(ecnt_done, t + 1)
                    V.reciprocal(ecnt[:, 1:2], ecnt[:, 0:1]).then_inc(ercp_done, 1)
                    dve.wait_ge(ercp_done, t + 1)
                    at_least(dve, turned, t)
                    V.tensor_scalar(emean[:], esum[:, 0:DE], ecnt[:, 1:2], None, ALU.mult).then_inc(emean_done, 1)
                if s == 1:
                    dve.wait_ge(l0_mm, t + 1)
                    dve.wait_ge(x_loaded, 16 * (t + 1))
                    V.scalar_tensor_tensor(r[:], l0_ps[0:NT, 0:D], dis[:, bass.ds(t, 1)], xt[:],
                                           ALU.mult, ALU.add).then_inc(r_done, 1)
                    dve.wait_ge(r_done, t + 1)
                    V.bn_stats(st1[:], r[:]).then_inc(stats1, 1)
                    dve.wait_ge(stats1, t + 1)
                    V.memset(carrier[:], 0.0)
                    V.bn_aggr(mv1[:], st1[:]).then_inc(var1, 1)
                    dve.wait_ge(std1, t + 1)
                    V.reciprocal(sd1[:, 1:2], sd1[:, 0:1]).then_inc(rstd1, 1)
                    dve.wait_ge(rstd1, t + 1)
                    V.tensor_scalar(y[:], r[:], mv1[:, 0:1], sd1[:, 1:2], ALU.subtract, ALU.mult).then_inc(y_done, 1)
                    dve.wait_ge(y_done, t + 1)
                    V.tensor_tensor(yb[:], y[:], b2_sb[:], ALU.add).then_inc(yb_done, 1)
                if s == 3:
                    dve.wait_ge(o_mm, t + 1)
                    dve.wait_ge(yb_done, t + 1)
                    V.tensor_tensor(z[:], o_ps[0:NT, 0:D], yb[:], ALU.add).then_inc(z_done, 1)
                    dve.wait_ge(z_done, t + 1)
                    V.bn_stats(st2[:], z[:]).then_inc(stats2, 1)
                    dve.wait_ge(stats2, t + 1)
                    V.memset(carrier[:], 0.0)
                    V.bn_aggr(mv2[:], st2[:]).then_inc(var2, 1)
                    dve.wait_ge(std2, t + 1)
                    V.reciprocal(sd2[:, 1:2], sd2[:, 0:1]).then_inc(rstd2, 1)
                    dve.wait_ge(rstd2, t + 1)
                    at_least(dve, out_stored, 16 * t)
                    V.tensor_scalar(o_sb[:], z[:], mv2[:, 0:1], sd2[:, 1:2], ALU.subtract, ALU.mult).then_inc(o_done, 1)

            def wide_window(n, w, k):
                p, g = shape_of(n)
                at_least(dve, wide_mm, k)
                at_least(dve, base_moved, k + n + 1)
                V.tensor_tensor(oh_wide[0:p, 0:g, :], dst_f[0:p, 0:g].unsqueeze(2).to_broadcast([p, g, WIDE]),
                                iota_win[0:p, :].unsqueeze(1).to_broadcast([p, g, WIDE]),
                                ALU.is_equal).then_inc(wide_oh, 1)
                dve.wait_ge(wide_oh, k + 1)
                V.tensor_scalar(dst_f[0:p, 0:g], dst_f[0:p, 0:g], float(-WIDE), None, ALU.add).then_inc(base_moved, 1)
                dve.wait_ge(wide_mm, k + 1)
                at_least(dve, wide_add, k)
                for c in range(KC):
                    to = aggT[:, c, bass.ds(w * WIDE, WIDE)]
                    last = V.tensor_tensor(to, to, agg_ps[c][:, :], ALU.add)
                last.then_inc(wide_add, 1)

            def general_group(n):
                p, g = shape_of(n)
                k0 = n * WINDOWS
                at_least(dve, base_moved, n * (WINDOWS + 1))
                V.tensor_copy(dst_f[0:p, 0:g], dst_all[0:p, n, 0:g]).then_inc(base_moved, 1)
                wide_window(n, 0, k0)
                with dve.Fori(1, WINDOWS) as w:
                    wide_window(n, w, k0 + w)

            by_flag(dve,
                    lambda: node_pass(dve, fast_step, dense, lambda: add_window(NG - 1, (NG - 1) % 2)),
                    lambda: general_pass(dve, general_group, dense))

        @block.tensor
        def _(pe):
            T = nc.tensor
            pe.wait_ge(pool_consts, 7)
            pe.wait_ge(consts, 2)
            pe.wait_ge(based, 1)
            T.matmul(setup_ps[:, 0:NG], ones[0:1, :], base_f[:], start=True, stop=True).then_inc(base_bc, 1)
            pe.wait_ge(check_step, 7)
            T.transpose(setup_ps[0:1, 0:P], worst[:, 2:3], ident[:]).then_inc(worst_T, 1)

            def spread(n, i, s):
                p, g = shape_of(n)
                pe.wait_ge(src_copied, n + 1)
                at_least(pe, same_done, n - 1)
                for k in range(g):
                    last = T.matmul(src_ps[s % 2][0:p, k * P:k * P + p], srcs[0:p, s, k:k + 1].to_broadcast([p, p]),
                                    ident[0:p, 0:p], start=True, stop=True)
                last.then_inc(src_spread, 1)

            def add_same(n, i, s):
                p, g = shape_of(n)
                b = s % 2
                pe.wait_ge(same_done, n + 1)
                pe.wait_ge(attr_in[s], 16 * (i + 1))
                at_least(pe, staged, n - 1)
                at_least(pe, idx_done, n - 1)
                for k in range(g):
                    T.matmul(sum_ps[b][0:p, k * ROW:k * ROW + DE], same[0:p, b, k, 0:p], attr[0:p, s, k, :],
                             start=True, stop=True)
                    T.matmul(sum_ps[b][0:p, k * ROW + DE:(k + 1) * ROW], same[0:p, b, k, 0:p], ones[0:p, 0:1],
                             start=True, stop=True)
                pe.wait_ge(earlier_done, n + 1)
                for k in range(g):
                    last = T.matmul(rep_ps[b][0:p, k:k + 1], earlier[0:p, b, k, 0:p], ones_b[0:p, :],
                                    start=True, stop=True)
                last.then_inc(summed, 1)

            def deg_count(m, b, first, final):
                pe.wait_ge(deg_oh, m + 1)
                for g in range(G):
                    last = T.matmul(deg_ps[0:HI, 0:P], oh_hi[:, b, g, :], oh_lo[:, b, g, :],
                                    start=first and g == 0, stop=final and g == G - 1)
                last.then_inc(deg_mm, 1)

            def edge_step(n, i, s, kind):
                spread(n, i, s)
                if not isinstance(n, int) or n > 0:
                    add_same(n - 1, i if s > 0 else i - 1, (s - 1) % 4)
                if kind == "deg":
                    deg_count(2 * n, 0, isinstance(n, int) and n == 0, False)
                    deg_count(2 * n + 1, 1, False, isinstance(n, int) and 2 * n + 1 == NG - 1)

            def turn_dis():
                pe.wait_ge(dis_loaded, 16)
                T.transpose(setup_ps[0:NT, 256:256 + TILES], dis_t[:], ident[0:TILES, 0:TILES]).then_inc(dis_turned, 1)

            edge_pass(pe, edge_step, turn_dis, nothing, lambda: add_same(NG - 1, ITER - 1, (NG - 1) % 4))

            pe.wait_ge(weights_in, 16 * 8)
            for j in range(HC):
                last = T.matmul(setup_ps[:, 400 + j:401 + j], W1u_sb[:, j * P:(j + 1) * P], u_sb[:], start=True, stop=True)
            last.then_inc(bias_mm, 1)
            pe.wait_ge(staged, NG)
            pe.wait_ge(idx_done, NG)
            pe.wait_ge(bias_done, 1)

            def sum_window(n, i, s):
                p, g = shape_of(n)
                b = s % 2
                pe.wait_ge(gathered[s], 16 * (G * i + g))
                pe.wait_ge(oh_ready, n + 1)
                at_least(pe, agg_added, n - 1)
                for c in range(KC):
                    for k in range(g):
                        last = T.matmul(agg_ps[b][:, c * WIN:(c + 1) * WIN], rows[0:p, s, k, c * P:(c + 1) * P],
                                        oh[0:p, b, k, :], start=k == 0, stop=k == g - 1)
                last.then_inc(agg_mm, 1)

            def dense(t, s, adds):
                if s == 0:
                    pe.wait_ge(aggw_ready, t + 1)
                    at_least(pe, r_done, t)
                    for c in range(KC):
                        last = T.matmul(l0_ps[0:NT, 0:D], aggw[:, c, :], W_sb[:, c, :], start=c == 0, stop=c == KC - 1)
                    last.then_inc(l0_mm, 1)
                if s == 1:
                    pe.wait_ge(y_done, t + 1)
                    pe.wait_ge(emean_done, t + 1)
                    at_least(pe, turned_out, 2 * t)
                    for c in range(KC):
                        T.transpose(tr_ps[:, c * NT:(c + 1) * NT], y[:, c * P:(c + 1) * P], ident[0:NT, 0:NT])
                    T.transpose(tr_ps[0:DE, KC * NT:(KC + 1) * NT], emean[:], ident[0:NT, 0:NT]).then_inc(turned, 1)
                if s == 2:
                    pe.wait_ge(turned_out, 2 * (t + 1))
                    at_least(pe, h_relu, t)
                    for j in range(HC):
                        for c in range(KC):
                            T.matmul(h_ps[:, j * NT:(j + 1) * NT], W1_sb[:, c, j * P:(j + 1) * P], yT[:, c, :],
                                     start=c == 0, stop=False)
                        last = T.matmul(h_ps[:, j * NT:(j + 1) * NT], W1e_sb[:, j * P:(j + 1) * P], eT[:],
                                        start=False, stop=True)
                    last.then_inc(h_mm, 1)
                if s == 3:
                    pe.wait_ge(h_relu, t + 1)
                    at_least(pe, z_done, t)
                    for j in range(HC):
                        last = T.matmul(o_ps[0:NT, 0:D], hT[:, j, :], W2_sb[:, j, :], start=j == 0, stop=j == HC - 1)
                    last.then_inc(o_mm, 1)

            def wide_window(n, k):
                p, g = shape_of(n)
                pe.wait_ge(wide_oh, k + 1)
                at_least(pe, wide_add, k)
                for c in range(KC):
                    for j in range(g):
                        last = T.matmul(agg_ps[c][:, :], rows[0:p, 0, j, c * P:(c + 1) * P], oh_wide[0:p, j, :],
                                        start=j == 0, stop=j == g - 1)
                last.then_inc(wide_mm, 1)

            def general_group(n):
                pe.wait_ge(gathered[0], 16 * G * (n + 1) if shape_of(n)[1] == G else 16 * (G * n + 1))
                wide_window(n, n * WINDOWS)
                with pe.Fori(1, WINDOWS) as w:
                    wide_window(n, n * WINDOWS + w)

            by_flag(pe,
                    lambda: node_pass(pe, sum_window, dense, nothing),
                    lambda: general_pass(pe, general_group, dense))


_INS = ['x', 'src', 'dst', 'edge_attr_64', 'L0_gnn_W', 'L1_gnn_u', 'L1_gnn_W1', 'L1_gnn_b1', 'L1_gnn_W2', 'L1_gnn_b2']


def kernel(**inputs):
    import numpy as _np
    import concourse.bacc as _bacc
    from concourse import mybir as _mybir
    from concourse.bass_utils import run_bass_kernel_spmd as _run

    nc = _bacc.Bacc("TRN2", target_bir_lowering=False, num_devices=1)
    arrays, args = {}, []
    for name in _INS:
        a = _np.ascontiguousarray(inputs[name])
        arrays[f"in_{name}_dram"] = a
        args.append(nc.dram_tensor(f"in_{name}_dram", a.shape, _mybir.dt.from_np(a.dtype), kind="ExternalInput").ap())
    out = nc.dram_tensor("out_0_dram", inputs['x'].shape, _mybir.dt.float32, kind="ExternalOutput").ap()
    gnn_kernel(nc, *args, out)
    r = _run(nc, [arrays], core_ids=[0])
    return r.results[0]["out_0_dram"]
```

```python
import concourse.bass as bass
from concourse import mybir
from contextlib import ExitStack

F32 = mybir.dt.float32
BF16 = mybir.dt.bfloat16
I32 = mybir.dt.int32
ALU = mybir.AluOpType
ACT = mybir.ActivationFunctionType
AX = mybir.AxisListType

P = 128
G = 4
GE = P * G
TABLES = 4
WIN = 64
WIDE = 512
NT = 125
LAG = 5
EPS = 1e-5


def gnn_kernel(nc, x, src, dst, edge_attr, W, u, W1, b1, W2, b2, out):
    N, D = x.shape
    E, DE = edge_attr.shape
    H = W1.shape[1]
    DG = u.shape[1]
    KC = D // P
    HC = H // P
    FULL = E // GE
    TAIL = E - FULL * GE
    NG = FULL + 1
    ITER = NG // G
    TILES = N // NT
    HI = (N + P - 1) // P
    ROW = DE + 1
    SPAN = (N + WIDE - 1) // WIDE * WIDE
    WINDOWS = SPAN // WIDE
    EROWS = (N + P + P - 1) // P * P
    HALF = ITER // 2
    XS = 2
    XC = TILES // XS
    PARTS = 3
    DP = PARTS * D
    CH = NG // 4
    BIG = 256.0
    assert NG % G == 0 and 0 < TAIL <= P and TILES * NT == N and ITER % 2 == 0
    assert D == KC * P and H == HC * P and DG == P and SPAN >= N + WIN
    ZERO = KC * SPAN // XC
    assert HALF + XC < ITER - 1 and TILES >= ITER - 1 - LAG and TILES == XC * XS
    assert CH <= P and CH * 4 == NG and ZERO * XC == KC * SPAN and ZERO >= EROWS // P * 5 and BIG > P

    etab = [nc.dram_tensor(f"edge_table{k}", (EROWS, ROW), F32, kind="Internal").ap() for k in range(TABLES)]
    xs_dram = nc.dram_tensor("x_scaled", (N, DP), BF16, kind="Internal").ap()
    dis_dram = nc.dram_tensor("dis", (HI * P,), F32, kind="Internal").ap()

    with ExitStack() as ctx:
        def sb(name, shape, dt=F32):
            return ctx.enter_context(nc.sbuf_tensor(name, shape, dt))

        def sem(name):
            return ctx.enter_context(nc.semaphore(name))

        aggT = sb("aggT", [P, KC, SPAN])
        src_f = sb("src_f", [P, NG, G])
        dst_f = sb("dst_f", [P, NG, G])
        src_parts = sb("src_parts", [P, NG, 2, G], BF16)
        rel = sb("rel", [P, NG, G])
        dst_hi = sb("dst_hi", [P, NG, G], BF16)
        dst_lo = sb("dst_lo", [P, NG, G], BF16)
        base_f = sb("base_f", [1, NG])
        base_i = sb("base_i", [1, NG], I32)
        worst = sb("worst", [P, 4])
        flag_f = sb("flag_f", [1, 1])
        flag = sb("flag", [1, 1], I32)

        ident = sb("ident", [P, P])
        ident_b = sb("ident_b", [P, P], BF16)
        weight = sb("weight", [P, P])
        iota_rep = sb("iota_rep", [P, P, G], BF16)
        iota_win = sb("iota_win", [P, WIDE])
        ones = sb("ones", [P, P])
        ones_b = sb("ones_b", [P, 1], BF16)
        junk = sb("junk", [P, 1])
        eps = sb("eps", [P, 1])
        zeros = sb("zeros", [P, ZERO])

        srcs = sb("srcs", [P, 4, 2, G], BF16)
        rows = sb("rows", [P, 4, G, DP], BF16)
        spare = sb("spare", [P, G, WIDE])

        def share(whole, offset, shape, dt=F32):
            free = 1
            for k in shape[1:]:
                free *= k
            words = free * mybir.dt.size(dt) // 4
            view = whole[0:shape[0], offset:offset + words]
            if dt != F32:
                view = view.bitcast(dt)
            if len(shape) == 3:
                view = view.rearrange("p (a b) -> p a b", b=shape[2])
            if len(shape) == 4:
                view = view.rearrange("p (a b c) -> p a b c", b=shape[2], c=shape[3])
            return view, offset + words

        rows_w = rows[:].rearrange("p s g d -> p (s g d)").bitcast(F32)
        spare_w = spare[:].rearrange("p g w -> p (g w)")
        agg_w = aggT[:].rearrange("p c n -> p (c n)")
        attr, used = share(rows_w, 0, [P, 4, G, DE])
        same, used = share(rows_w, used, [P, 2, G, P])
        stage, used = share(rows_w, used, [P, 4, G, ROW])
        xs_in, used = share(rows_w, used, [NT, XS, D])
        xs_rest, used = share(rows_w, used, [NT, XS, D])
        xs_out, used = share(rows_w, used, [NT, XS, DP], BF16)
        earlier, used = share(spare_w, 0, [P, 2, G, P], BF16)
        oh_hi, used = share(spare_w, used, [P, 2, HI * G], BF16)
        oh_lo, used = share(spare_w, used, [P, 2, P * G], BF16)
        oh_wide, used = share(spare_w, 0, [P, G, WIDE], BF16)
        raw_i, used = share(agg_w, 0, [CH, 2 * 4, GE], I32)
        raw_f, used = share(agg_w, used, [CH, 2 * 4, GE])
        dst_i, used = share(agg_w, used, [P, NG * G], I32)
        digit_i, used = share(agg_w, used, [P, 2, NG * G], I32)
        due, used = share(agg_w, used, [P, NG])
        late, used = share(agg_w, used, [P, NG])
        rep = sb("rep", [P, 2, G])
        eidx = sb("eidx", [P, 4, G], I32)
        deg = sb("deg", [HI, P])
        dmask = sb("dmask", [HI, P])
        dsq = sb("dsq", [HI, P])
        dinv = sb("dinv", [HI, P])
        dis_h = sb("dis_h", [HI, P])
        dis_t = sb("dis_t", [TILES, NT])
        dis = sb("dis_nodes", [NT, TILES])
        gidx = sb("gidx", [P, 4, G], I32)
        oh = sb("oh", [P, 2, G, WIN], BF16)
        dst_w = sb("dst_w", [P, G])
        W_sb = sb("W_sb", [P, KC, D])
        W1_sb = sb("W1_sb", [P, KC, H])
        W1e_sb = sb("W1e_sb", [DE, H])
        W1u_sb = sb("W1u_sb", [DG, H])
        W2_sb = sb("W2_sb", [P, HC, D])
        b1_sb = sb("b1_sb", [P, HC])
        b2_sb = sb("b2_sb", [NT, D])
        u_sb = sb("u_sb", [DG, 1])
        hbias = sb("hbias", [P, HC])
        aggw = sb("aggw", [P, KC, NT])
        xt = sb("xt", [NT, D])
        et = sb("et", [NT, TABLES, ROW])
        esum = sb("esum", [NT, ROW])
        ecnt = sb("ecnt", [NT, 2])
        emean = sb("emean", [NT, DE])
        r = sb("r", [NT, D])
        y = sb("y", [NT, D])
        yb = sb("yb", [NT, D])
        z = sb("z", [NT, D])
        o_sb = sb("o_sb", [NT, D])
        carrier = sb("carrier", [1, 1])
        st1 = sb("st1", [NT, 6])
        mv1 = sb("mv1", [NT, 2])
        sd1 = sb("sd1", [NT, 2])
        st2 = sb("st2", [NT, 6])
        mv2 = sb("mv2", [NT, 2])
        sd2 = sb("sd2", [NT, 2])
        yT = sb("yT", [P, KC, NT])
        eT = sb("eT", [DE, NT])
        hT = sb("hT", [P, HC, NT])

        bank = [ctx.enter_context(nc.psum_tensor(f"bank{k}", [P, 512], F32)) for k in range(8)]
        src_ps = bank[0:2]
        sum_ps = bank[2:4]
        deg_ps = bank[4]
        agg_ps = bank[5:7]
        setup_ps = bank[7]
        l0_ps, tr_ps, h_ps, o_ps = bank[2], bank[3], bank[4], bank[7]
        rep_ps = agg_ps

        idx_in, weights_in = [sem("src_in"), sem("dst_in")], sem("weights_in")
        attr_in = [sem(f"attr_in{s}") for s in range(4)]
        xs_loaded, xs_stored, dis_stored, dis_loaded = sem("xs_loaded"), sem("xs_stored"), sem("dis_stored"), sem("dis_loaded")
        tables_zero, zeros_ready = [sem(f"table_zero{k}") for k in range(TABLES)], sem("zeros_ready")
        scattered = [sem(f"scattered{k}") for k in range(TABLES)]
        gathered = [sem(f"gathered{s}") for s in range(4)]
        x_loaded, e_loaded, out_stored = sem("x_loaded"), sem("e_loaded"), sem("out_stored")
        consts, pool_consts, padded, converted = sem("consts"), sem("pool_consts"), sem("padded"), [sem("src_conv"), sem("dst_conv")]
        idx_turned, src_laid, dst_laid, src_high, src_split, dst_split = (
            [sem("src_turned"), sem("dst_turned")], sem("src_laid"), sem("dst_laid"), sem("src_high"), sem("src_split"),
            sem("dst_split"))
        xs_high, xs_left, xs_mid, xs_low = sem("xs_high"), sem("xs_left"), sem("xs_mid"), sem("xs_low")
        based, base_bc, rel_done, check_step, worst_T, flag_ready = (
            sem("based"), sem("base_bc"), sem("rel_done"), sem("check_step"), sem("worst_T"), sem("flag_ready"))
        bias_mm, bias_done = sem("bias_mm"), sem("bias_done")
        src_copied, src_spread, same_done, earlier_done, summed, rep_done, idx_done, staged = (
            sem("src_copied"), sem("src_spread"), sem("same_done"), sem("earlier_done"), sem("summed"), sem("rep_done"),
            sem("idx_done"), sem("staged"))
        agg_cleared = sem("agg_cleared")
        deg_oh, deg_mm = sem("deg_oh"), sem("deg_mm")
        deg_step, deg_root, dis_turned, dis_ready = sem("deg_step"), sem("deg_root"), sem("dis_turned"), sem("dis_ready")
        gidx_ready, oh_ready, agg_mm, agg_added = sem("gidx_ready"), sem("oh_ready"), sem("agg_mm"), sem("agg_added")
        wide_oh, wide_mm, wide_add, base_moved = sem("wide_oh"), sem("wide_mm"), sem("wide_add"), sem("base_moved")
        aggw_ready, l0_mm, r_done, stats1, var1, std1, rstd1, y_done, yb_done = (
            sem("aggw_ready"), sem("l0_mm"), sem("r_done"), sem("stats1"), sem("var1"), sem("std1"), sem("rstd1"),
            sem("y_done"), sem("yb_done"))
        esum_done, ecnt_done, ercp_done, emean_done = sem("esum_done"), sem("ecnt_done"), sem("ercp_done"), sem("emean_done")
        turned, turned_out, h_mm, h_relu, o_mm = sem("turned"), sem("turned_out"), sem("h_mm"), sem("h_relu"), sem("o_mm")
        z_done, stats2, var2, std2, rstd2, o_done = (
            sem("z_done"), sem("stats2"), sem("var2"), sem("std2"), sem("rstd2"), sem("o_done"))

        def at_least(eng, s, count):
            if not (isinstance(count, int) and count <= 0):
                eng.wait_ge(s, count)

        def shape_of(n):
            return (TAIL, 1) if isinstance(n, int) and n == FULL else (P, G)

        def edge_rows(a, n):
            if isinstance(n, int) and n == FULL:
                return a[FULL * GE:E, :].rearrange("(p g) f -> p g f", g=1)
            return a[bass.ds(n * GE, GE), :].rearrange("(p g) f -> p g f", g=G)

        def edge_pass(eng, step, start, after, drain):
            def iteration(i, kind):
                for s in range(G):
                    step(4 * i + s, i, s, kind)
            iteration(0, "deg")
            with eng.Fori(1, HALF - 1) as i:
                iteration(i, "deg")
            iteration(HALF - 1, "deg")
            start()
            iteration(HALF, "xs")
            with eng.Fori(HALF + 1, HALF + XC) as i:
                iteration(i, "xs")
            after()
            for i in range(HALF + XC, ITER):
                iteration(i, "rest")
            drain()

        def nothing(*_):
            return None

        def node_pass(eng, step, dense, drain, last_norm=nothing):
            def iteration(i, t):
                for s in range(G):
                    step(4 * i + s, i, s)
                    if t is not None:
                        dense(t, s, 4 * i)
            iteration(0, None)
            with eng.Fori(1, LAG) as i:
                iteration(i, None)
            iteration(LAG, 0)
            with eng.Fori(LAG + 1, ITER - 1) as i:
                iteration(i, i - LAG)
            iteration(ITER - 1, ITER - 1 - LAG)
            drain()
            for t in range(ITER - LAG, TILES):
                for s in range(G):
                    dense(t, s, NG)
            last_norm(TILES - 1)

        def general_pass(eng, group, dense, finish=nothing, last_norm=nothing):
            group(0)
            with eng.Fori(1, FULL) as n:
                group(n)
            group(FULL)
            finish()
            for s in range(G):
                dense(0, s, None)
            with eng.Fori(1, TILES - 1) as t:
                for s in range(G):
                    dense(t, s, None)
            for s in range(G):
                dense(TILES - 1, s, None)
            last_norm(TILES - 1)

        def by_flag(eng, fast, general):
            eng.wait_ge(flag_ready, 1)
            ok = eng.value_load(flag[0:1, 0:1], min_val=0, max_val=1)
            with eng.If(ok == 1):
                fast()
            with eng.Else():
                general()

        block = ctx.enter_context(nc.Block())

        @block.sync
        def _(sp):
            main = FULL - 3 * CH
            with nc.allow_non_contiguous_dma(reason="small loads"):
                sp.wait_ge(padded, 1)
                for a, edges in enumerate((src, dst)):
                    sp.dma_start(raw_i[:, 4 * a:4 * a + 3, :], edges[0:3 * CH * GE].rearrange(
                        "(c n e) -> n c e", c=3, n=CH)).then_inc(idx_in[a], 16)
                    sp.dma_start(raw_i[0:main, 4 * a + 3, :], edges[3 * CH * GE:FULL * GE].rearrange(
                        "(n e) -> n e", n=main)).then_inc(idx_in[a], 16)
                    sp.dma_start(raw_i[main:main + 1, 4 * a + 3, 0:TAIL * G].rearrange("n (p g) -> n p g", g=G)[:, :, 0],
                                 edges[FULL * GE:E].rearrange("(n p) -> n p", n=1)).then_inc(idx_in[a], 16)

            def zero_table(k):
                blocks = ROW // 5
                sp.dma_start(etab[k].rearrange("(p r) f -> p (r f)", p=P).rearrange("p (b w) -> p b w", b=blocks),
                             zeros[:, 0:EROWS // P * 5].unsqueeze(1).to_broadcast([P, blocks, EROWS // P * 5])
                             ).then_inc(tables_zero[k], 16)

            def load_weights():
                xs_store(XC - 1)
                with nc.allow_non_contiguous_dma(reason="small loads"):
                    sp.dma_start(W_sb[:], W.rearrange("(c p) n -> p c n", p=P)).then_inc(weights_in, 16)
                    sp.dma_start(W1_sb[:], W1[0:D, :].rearrange("(c p) n -> p c n", p=P)).then_inc(weights_in, 16)
                    sp.dma_start(W1e_sb[:], W1[D:D + DE, :]).then_inc(weights_in, 16)
                    sp.dma_start(W1u_sb[:], W1[D + DE:D + DE + DG, :]).then_inc(weights_in, 16)
                    sp.dma_start(W2_sb[:], W2.rearrange("(c p) n -> p c n", p=P)).then_inc(weights_in, 16)
                    sp.dma_start(b1_sb[:], b1.rearrange("(c p) -> p c", p=P)).then_inc(weights_in, 16)
                    sp.dma_start(u_sb[:], u[0:1, :].rearrange("a d -> d a")).then_inc(weights_in, 16)
                    sp.dma_start(b2_sb[:], b2.rearrange("(a d) -> a d", a=1).partition_broadcast(NT)).then_inc(weights_in, 16)

            def attr_load(n, i, s, kind):
                p, g = shape_of(n)
                at_least(sp, summed, n - 3)
                sp.dma_start(attr[0:p, s, 0:g, :], edge_rows(edge_attr, n)).then_inc(attr_in[s], 16)
                if isinstance(i, int) and i == 0:
                    if s == 0:
                        sp.wait_ge(zeros_ready, 1)
                    zero_table(s)
                if kind == "xs" and s == 0:
                    c = i - HALF
                    if not isinstance(c, int) or c > 0:
                        xs_store(c - 1)
                    sp.dma_start(xs_in[:], xs_rows(x, c)).then_inc(xs_loaded, 16)

            def dis_round_trip():
                sp.wait_ge(deg_step, 4)
                sp.dma_start(dis_dram.rearrange("(h l) -> h l", l=P), dis_h[:]).then_inc(dis_stored, 16)
                sp.wait_ge(dis_stored, 16)
                sp.dma_start(dis_t[:], dis_dram[0:N].rearrange("(t p) -> t p", p=NT)).then_inc(dis_loaded, 16)

            def xs_rows(a, c):
                return a[bass.ds(c * (XS * NT), XS * NT), :].rearrange("(k p) d -> p k d", p=NT)

            def xs_store(c):
                sp.wait_ge(xs_low, c + 1)
                sp.dma_start(xs_rows(xs_dram, c), xs_out[:]).then_inc(xs_stored, 16)

            edge_pass(sp, attr_load, dis_round_trip, load_weights, nothing)

            for k in range(TABLES):
                sp.wait_ge(scattered[k], 16 * (NG if k == 0 else FULL))

            def load_nodes(t):
                at_least(sp, r_done, t)
                sp.dma_start(xt[:], x[bass.ds(t * NT, NT), :]).then_inc(x_loaded, 16)
                at_least(sp, esum_done, t)
                for k in range(TABLES):
                    sp.dma_start(et[:, k, :], etab[k][bass.ds(t * NT, NT), :]).then_inc(e_loaded, 16)

            def store_nodes(t):
                sp.wait_ge(o_done, t + 1)
                sp.dma_start(out[bass.ds(t * NT, NT), :], o_sb[:]).then_inc(out_stored, 16)

            load_nodes(0)
            with sp.Fori(1, TILES) as t:
                load_nodes(t)
                store_nodes(t - 1)
            store_nodes(TILES - 1)
            sp.wait_ge(out_stored, 16 * TILES)

        @block.gpsimd
        def _(pool):
            nc.gpsimd.memset(ones[:], 1.0).then_inc(pool_consts, 1)
            nc.gpsimd.iota(iota_rep[:], pattern=[[1, P], [0, G]], base=0, channel_multiplier=0,
                           allow_small_or_imprecise_dtypes=True).then_inc(pool_consts, 1)
            nc.gpsimd.iota(iota_win[:], pattern=[[1, WIDE]], base=0, channel_multiplier=0,
                           allow_small_or_imprecise_dtypes=True).then_inc(pool_consts, 1)
            nc.gpsimd.iota(junk[:], pattern=[[1, 1]], base=N, channel_multiplier=1,
                           allow_small_or_imprecise_dtypes=True).then_inc(pool_consts, 1)
            nc.gpsimd.iota(due[:], pattern=[[NT, ITER], [0, G]], base=-NT * (LAG - 1), channel_multiplier=0,
                           allow_small_or_imprecise_dtypes=True).then_inc(pool_consts, 1)
            nc.gpsimd.memset(weight[:], BIG).then_inc(pool_consts, 1)
            pool.wait_ge(pool_consts, 6)
            nc.gpsimd.affine_select(out=ident[:], in_=ones[:], compare_op=ALU.is_equal, fill=0.0, base=0,
                                    pattern=[[-1, P]], channel_multiplier=1).then_inc(pool_consts, 1)
            nc.gpsimd.affine_select(out=weight[:], in_=weight[:], compare_op=ALU.is_gt, fill=1.0, base=0,
                                    pattern=[[1, P]], channel_multiplier=-1).then_inc(pool_consts, 1)

            last_row, last_node = pool.to_reg(EROWS - 1), pool.to_reg(N - 1)

            def scatter(n, i, s, kind):
                p, tiles = shape_of(n)
                landed = pool.to_reg(16 * n) if not isinstance(n, int) else 16 * n
                filled = n + 1 if isinstance(n, int) else pool.to_reg(n + 1)
                pool.wait_ge(tables_zero[0], 16)
                pool.wait_ge(staged, filled)
                pool.wait_ge(idx_done, filled)
                for g in range(tiles):
                    pool.wait_ge(tables_zero[g], 16)
                    at_least(pool, scattered[g], landed)
                    pool.indirect_dma_start(
                        etab[g][:, :], bass.IndirectOffsetOnAxis(eidx[0:p, s, g:g + 1], 0),
                        stage[0:p, s, g, :], None, bounds_check=last_row, oob_is_err=True,
                        compute_op=ALU.add).then_inc(scattered[g], 16)

            edge_pass(pool, scatter, nothing, nothing, nothing)

            pool.wait_ge(summed, NG)
            for k in range(TABLES):
                pool.wait_ge(scattered[k], 16 * (NG if k == 0 else FULL))

            def gather(n, s):
                p, tiles = shape_of(n)
                copied = pool.to_reg(n + 1) if not isinstance(n, int) else n + 1
                pool.wait_ge(xs_stored, 16 * XC)
                pool.wait_ge(gidx_ready, copied)
                for g in range(tiles):
                    pool.indirect_dma_start(
                        rows[0:p, s, g, :], None, xs_dram[:, :],
                        bass.IndirectOffsetOnAxis(gidx[0:p, s, g:g + 1], 0),
                        bounds_check=last_node, oob_is_err=True).then_inc(gathered[s], 16)

            def fast_gather(n, i, s):
                at_least(pool, agg_mm, n - 3)
                gather(n, s)

            def general_gather(n):
                at_least(pool, wide_mm, n * WINDOWS)
                gather(n, 0)

            by_flag(pool,
                    lambda: node_pass(pool, fast_gather, nothing, nothing),
                    lambda: general_pass(pool, general_gather, nothing))

        @block.scalar
        def _(act):
            act.wait_ge(idx_in[0], 48)
            nc.scalar.copy(raw_f[:, 0:4, :], raw_i[:, 0:4, :]).then_inc(converted[0], 1)
            for c in range(4):
                act.wait_ge(idx_turned[0], c + 1)
                nc.scalar.copy(src_f[:, c * CH:(c + 1) * CH, :].rearrange("p n g -> p g n"),
                               bank[c][:, 0:G * CH].rearrange("p (g n) -> p g n", g=G)).then_inc(src_laid, 1)
            act.wait_ge(src_laid, 4)
            nc.scalar.copy(src_parts[:, :, 0, :], src_f[:]).then_inc(src_high, 1)
            act.wait_ge(src_split, 1)

            def copy_src(n, s):
                at_least(act, src_spread, n - 3)
                nc.scalar.copy(srcs[:, s, :, :], src_parts[:, n, :, :]).then_inc(src_copied, 1)

            def evacuate(n, i, s):
                p, g = shape_of(n)
                act.wait_ge(summed, n + 1)
                for k in range(g):
                    at_least(act, scattered[k], 16 * (n - 3))
                nc.scalar.copy(stage[0:p, s, 0:g, :].rearrange("p g f -> p (g f)"),
                               sum_ps[s % 2][0:p, 0:g * ROW]).then_inc(staged, 1)

            def edge_step(n, i, s, kind):
                if not isinstance(n, int) or n + 2 < NG:
                    copy_src(n + 2, (s + 2) % 4)
                if not isinstance(n, int) or n > 0:
                    evacuate(n - 1, i, (s - 1) % 4)
                if kind == "xs" and s >= 2:
                    scale(i - HALF, s)

            def scale(c, s):
                if s == 2:
                    act.wait_ge(xs_loaded, 16 * (c + 1))
                    at_least(act, xs_stored, 16 * c)
                    for k in range(XS):
                        last = nc.scalar.activation(xs_out[:, k, 0:D], xs_in[:, k, :], ACT.Copy,
                                                    scale=dis[:, bass.ds(c * XS + k, 1)])
                    last.then_inc(xs_high, 1)
                else:
                    act.wait_ge(xs_left, c + 1)
                    nc.scalar.copy(xs_out[:, :, D:2 * D], xs_rest).then_inc(xs_mid, 1)

            def roots():
                act.wait_ge(deg_step, 1)
                nc.scalar.activation(dsq[:], deg[:], ACT.Sqrt).then_inc(deg_root, 1)
                act.wait_ge(dis_ready, 1)

            copy_src(0, 0)
            copy_src(1, 1)
            edge_pass(act, edge_step, roots, nothing, lambda: evacuate(NG - 1, None, (NG - 1) % 4))

            def copy_idx(n, s):
                p, g = shape_of(n)
                nc.scalar.copy(gidx[0:p, s, 0:g], src_f[0:p, n, 0:g]).then_inc(gidx_ready, 1)

            def fast_step(n, i, s):
                m, sm = n + 3, (s + 3) % 4
                if isinstance(m, int) and m >= NG:
                    return
                at_least(act, gathered[sm], 16 * G * (i if s == 0 else i + 1))
                copy_idx(m, sm)

            def last_norm(t):
                act.wait_ge(var2, t + 1)
                nc.scalar.activation(sd2[:, 0:1], mv2[:, 1:2], ACT.Sqrt, bias=eps[0:NT, :]).then_inc(std2, 1)

            def dense(t, s, adds):
                if s == 0:
                    if adds is not None:
                        at_least(act, agg_added, adds)
                    at_least(act, l0_mm, t)
                    nc.scalar.copy(aggw[:], aggT[:, :, bass.ds(t * NT, NT)]).then_inc(aggw_ready, 1)
                    if not isinstance(t, int) or t > 0:
                        last_norm(t - 1)
                    act.wait_ge(var1, t + 1)
                    nc.scalar.activation(sd1[:, 0:1], mv1[:, 1:2], ACT.Sqrt, bias=eps[0:NT, :]).then_inc(std1, 1)
                if s == 2:
                    act.wait_ge(turned, t + 1)
                    nc.scalar.copy(yT[:].rearrange("p c n -> p (c n)"), tr_ps[:, 0:KC * NT]).then_inc(turned_out, 1)
                    nc.scalar.copy(eT[:], tr_ps[0:DE, KC * NT:(KC + 1) * NT]).then_inc(turned_out, 1)
                if s == 3:
                    act.wait_ge(h_mm, t + 1)
                    at_least(act, o_mm, t)
                    for j in range(HC):
                        last = nc.scalar.activation(hT[:, j, :], h_ps[:, j * NT:(j + 1) * NT], ACT.Relu,
                                                    bias=hbias[:, j:j + 1])
                    last.then_inc(h_relu, 1)

            def general_group(n):
                at_least(act, wide_mm, n * WINDOWS)
                copy_idx(n, 0)

            def fast():
                copy_idx(0, 0)
                copy_idx(1, 1)
                copy_idx(2, 2)
                node_pass(act, fast_step, dense, nothing, last_norm)

            act.wait_ge(bias_done, 1)
            by_flag(act, fast, lambda: general_pass(act, general_group, dense,
                                                     lambda: act.wait_ge(wide_add, NG * WINDOWS), last_norm))

        @block.vector
        def _(dve):
            V = nc.vector
            V.memset(raw_i[:].rearrange("n (a c) e -> n a c e", a=2)[:, :, 3, :], -1).then_inc(padded, 1)
            V.memset(zeros[:], 0.0).then_inc(zeros_ready, 1)
            V.memset(ones_b[:], 1.0).then_inc(consts, 1)
            V.memset(eps[:], EPS).then_inc(consts, 1)
            dve.wait_ge(pool_consts, 8)
            V.tensor_copy(ident_b[:], ident[:]).then_inc(consts, 1)
            dve.wait_ge(idx_in[1], 48)
            V.tensor_copy(raw_f[:, 4:8, :], raw_i[:, 4:8, :]).then_inc(converted[1], 1)
            dve.wait_ge(src_high, 1)
            V.tensor_tensor(src_parts[:, :, 1, :], src_f[:], src_parts[:, :, 0, :], ALU.subtract).then_inc(src_split, 1)
            for c in range(4):
                dve.wait_ge(idx_turned[1], c + 1)
                V.tensor_copy(dst_f[:, c * CH:(c + 1) * CH, :].rearrange("p n g -> p g n"),
                              bank[4 + c][:, 0:G * CH].rearrange("p (g n) -> p g n", g=G)).then_inc(dst_laid, 1)
            dve.wait_ge(dst_laid, 4)
            V.tensor_copy(dst_i, dst_f[:].rearrange("p n g -> p (n g)")).then_inc(dst_split, 1)
            V.tensor_copy(base_f[:], dst_f[0:1, :, 0]).then_inc(based, 1)
            V.tensor_copy(base_i[:], dst_f[0:1, :, 0]).then_inc(based, 1)
            dve.wait_ge(dst_split, 1)
            V.tensor_scalar(digit_i[:, 0, :], dst_i, 7, None, ALU.arith_shift_right).then_inc(dst_split, 1)
            V.tensor_scalar(digit_i[:, 1, :], dst_i, P - 1, None, ALU.bitwise_and).then_inc(dst_split, 1)
            dve.wait_ge(dst_split, 3)
            V.tensor_copy(dst_hi[:].rearrange("p n g -> p (n g)"), digit_i[:, 0, :]).then_inc(dst_split, 1)
            V.tensor_copy(dst_lo[:].rearrange("p n g -> p (n g)"), digit_i[:, 1, :]).then_inc(dst_split, 1)
            dve.wait_ge(base_bc, 1)
            V.tensor_tensor(rel[:], dst_f[:], setup_ps[:, 0:NG].unsqueeze(2).to_broadcast([P, NG, G]),
                            ALU.subtract).then_inc(rel_done, 1)
            V.tensor_tensor(late[:], due[:], setup_ps[:, 0:NG], ALU.subtract).then_inc(check_step, 1)
            q = spare_w[:, 0:NG * G].rearrange("p (n g) -> p n g", g=G)
            V.memset(q[:, FULL, :], -1.0).then_inc(check_step, 1)
            dve.wait_ge(rel_done, 1)
            dve.wait_ge(check_step, 2)
            V.scalar_tensor_tensor(q[:, 0:FULL, :], rel[:, 0:FULL, :], float(1 - WIN), rel[:, 0:FULL, :],
                                   ALU.add, ALU.mult).then_inc(check_step, 1)
            V.scalar_tensor_tensor(q[0:TAIL, FULL, 0:1], rel[0:TAIL, FULL, 0:1], float(1 - WIN),
                                   rel[0:TAIL, FULL, 0:1], ALU.add, ALU.mult).then_inc(check_step, 1)
            dve.wait_ge(check_step, 4)
            V.tensor_reduce(worst[:, 0:1], q, AX.XY, ALU.max).then_inc(check_step, 1)
            V.tensor_reduce(worst[:, 1:2], late[:], AX.X, ALU.max).then_inc(check_step, 1)
            dve.wait_ge(check_step, 6)
            V.tensor_tensor(worst[:, 2:3], worst[:, 0:1], worst[:, 1:2], ALU.max).then_inc(check_step, 1)
            dve.wait_ge(worst_T, 1)
            V.tensor_reduce(flag_f[:], setup_ps[0:1, 0:P], AX.X, ALU.max).then_inc(check_step, 1)
            dve.wait_ge(check_step, 8)
            V.tensor_scalar(flag[:], flag_f[:], 0.0, None, ALU.is_le).then_inc(flag_ready, 1)

            def compare(n, i, s):
                p, g = shape_of(n)
                dve.wait_ge(src_spread, n + 1)
                at_least(dve, summed, n - 1)
                b = s % 2
                V.tensor_tensor(same[0:p, b, 0:g, 0:p],
                                src_ps[b][0:p, :].rearrange("p (g e) -> p g e", g=G)[:, 0:g, 0:p],
                                src_f[0:p, n, 0:g].unsqueeze(2).to_broadcast([p, g, p]),
                                ALU.is_equal).then_inc(same_done, 1)
                dve.wait_ge(same_done, n + 1)
                V.tensor_tensor(earlier[0:p, b, 0:g, 0:p], same[0:p, b, 0:g, 0:p],
                                weight[0:p, 0:p].unsqueeze(1).to_broadcast([p, g, p]),
                                ALU.mult).then_inc(earlier_done, 1)

            def index(n, i, s):
                p, g = shape_of(n)
                dve.wait_ge(summed, n + 1)
                V.tensor_scalar(rep[0:p, s % 2, 0:g], rep_ps[s % 2][0:p, 0:g], BIG,
                                junk[0:p, :], ALU.is_ge, ALU.mult).then_inc(rep_done, 1)
                for k in range(g):
                    at_least(dve, scattered[k], 16 * (n - 3))
                dve.wait_ge(rep_done, n + 1)
                V.tensor_tensor(eidx[0:p, s, 0:g], rep[0:p, s % 2, 0:g], src_f[0:p, n, 0:g],
                                ALU.max).then_inc(idx_done, 1)

            def deg_one_hot(m, b):
                at_least(dve, deg_mm, m - 1)
                for digit, to, count in ((dst_hi, oh_hi, HI), (dst_lo, oh_lo, P)):
                    last = V.tensor_tensor(to[:, b, :].rearrange("p (v g) -> p v g", g=G),
                                           digit[:, m, :].unsqueeze(1).to_broadcast([P, count, G]),
                                           iota_rep[:, 0:count, :], ALU.is_equal)
                last.then_inc(deg_oh, 1)

            def split_scaled(c, s):
                if s == 2:
                    dve.wait_ge(xs_high, c + 1)
                    at_least(dve, xs_mid, c)
                    at_least(dve, xs_low, c)
                    for k in range(XS):
                        last = V.scalar_tensor_tensor(xs_rest[:, k, :], xs_in[:, k, :], dis[:, bass.ds(c * XS + k, 1)],
                                                      xs_out[:, k, 0:D], ALU.mult, ALU.subtract)
                    last.then_inc(xs_left, 1)
                else:
                    dve.wait_ge(xs_mid, c + 1)
                    V.tensor_tensor(xs_out[:, :, 2 * D:3 * D], xs_rest, xs_out[:, :, D:2 * D],
                                    ALU.subtract).then_inc(xs_low, 1)

            def edge_step(n, i, s, kind):
                compare(n, i, s)
                if kind == "deg":
                    deg_one_hot(2 * n, 0)
                if not isinstance(n, int) or n > 0:
                    index(n - 1, i, (s - 1) % 4)
                if kind == "deg":
                    deg_one_hot(2 * n + 1, 1)
                if kind == "xs" and s == 0:
                    V.tensor_copy(agg_w[:, bass.ds((i - HALF) * ZERO, ZERO)], zeros[:]).then_inc(agg_cleared, 1)
                if kind == "xs" and s >= 2:
                    split_scaled(i - HALF, s)

            def degree_factors():
                dve.wait_ge(deg_mm, NG)
                V.tensor_scalar(deg[:], deg_ps[0:HI, 0:P], 1.0, None, ALU.max).then_inc(deg_step, 1)
                V.tensor_scalar(dmask[:], deg_ps[0:HI, 0:P], 0.0, None, ALU.is_gt).then_inc(deg_step, 1)
                dve.wait_ge(deg_root, 1)
                V.reciprocal(dinv[:], dsq[:]).then_inc(deg_step, 1)
                dve.wait_ge(deg_step, 3)
                V.tensor_tensor(dis_h[:], dinv[:], dmask[:], ALU.mult).then_inc(deg_step, 1)
                dve.wait_ge(dis_turned, 1)
                V.tensor_copy(dis[:], setup_ps[0:NT, 256:256 + TILES]).then_inc(dis_ready, 1)

            dve.wait_ge(dst_split, 5)
            dve.wait_ge(idx_turned[0], 4)
            edge_pass(dve, edge_step, degree_factors, nothing, lambda: index(NG - 1, None, (NG - 1) % 4))

            dve.wait_ge(agg_cleared, XC)
            dve.wait_ge(bias_mm, 1)
            V.tensor_tensor(hbias[:], setup_ps[:, 400:400 + HC], b1_sb[:], ALU.add).then_inc(bias_done, 1)

            def one_hot(n, b):
                p, g = shape_of(n)
                at_least(dve, agg_mm, n - 1)
                V.tensor_tensor(oh[0:p, b, 0:g, :], rel[0:p, n, 0:g].unsqueeze(2).to_broadcast([p, g, WIN]),
                                iota_win[0:p, 0:WIN].unsqueeze(1).to_broadcast([p, g, WIN]),
                                ALU.is_equal).then_inc(oh_ready, 1)

            def add_window(n, b):
                base = dve.value_load(base_i[0:1, bass.ds(n, 1)], min_val=0, max_val=N - 1)
                dve.wait_ge(agg_mm, n + 1)
                at_least(dve, agg_added, n)
                to = aggT[:, :, bass.ds(base, WIN)]
                V.tensor_tensor(to, to, agg_ps[b][:, 0:KC * WIN].rearrange("p (c w) -> p c w", c=KC),
                                ALU.add).then_inc(agg_added, 1)

            def fast_step(n, i, s):
                if not isinstance(n, int) or n + 1 < NG:
                    one_hot(n + 1, (s + 1) % 2)
                if s > 0:
                    add_window(n - 1, (s + 1) % 2)
                if s == 3:
                    add_window(n, s % 2)

            def fast():
                one_hot(0, 0)
                node_pass(dve, fast_step, dense, nothing, last_norm)

            def last_norm(t):
                dve.wait_ge(std2, t + 1)
                V.reciprocal(sd2[:, 1:2], sd2[:, 0:1]).then_inc(rstd2, 1)
                dve.wait_ge(rstd2, t + 1)
                at_least(dve, out_stored, 16 * t)
                V.tensor_scalar(o_sb[:], z[:], mv2[:, 0:1], sd2[:, 1:2], ALU.subtract, ALU.mult).then_inc(o_done, 1)

            def dense(t, s, adds):
                if s == 0:
                    dve.wait_ge(l0_mm, t + 1)
                    dve.wait_ge(x_loaded, 16 * (t + 1))
                    V.scalar_tensor_tensor(r[:], l0_ps[0:NT, 0:D], dis[:, bass.ds(t, 1)], xt[:],
                                           ALU.mult, ALU.add).then_inc(r_done, 1)
                    dve.wait_ge(e_loaded, 16 * TABLES * (t + 1))
                    V.tensor_reduce(esum[:], et[:].rearrange("p k f -> p f k"), AX.X, ALU.add).then_inc(esum_done, 1)
                    dve.wait_ge(r_done, t + 1)
                    V.bn_stats(st1[:], r[:]).then_inc(stats1, 1)
                    dve.wait_ge(esum_done, t + 1)
                    V.tensor_scalar(ecnt[:, 0:1], esum[:, DE:ROW], 1.0, None, ALU.max).then_inc(ecnt_done, 1)
                    dve.wait_ge(stats1, t + 1)
                    V.memset(carrier[:], 0.0)
                    V.bn_aggr(mv1[:], st1[:]).then_inc(var1, 1)
                    dve.wait_ge(ecnt_done, t + 1)
                    V.reciprocal(ecnt[:, 1:2], ecnt[:, 0:1]).then_inc(ercp_done, 1)
                    dve.wait_ge(ercp_done, t + 1)
                    at_least(dve, turned, t)
                    V.tensor_scalar(emean[:], esum[:, 0:DE], ecnt[:, 1:2], None, ALU.mult).then_inc(emean_done, 1)
                    dve.wait_ge(std1, t + 1)
                    V.reciprocal(sd1[:, 1:2], sd1[:, 0:1]).then_inc(rstd1, 1)
                    dve.wait_ge(rstd1, t + 1)
                    V.tensor_scalar(y[:], r[:], mv1[:, 0:1], sd1[:, 1:2], ALU.subtract, ALU.mult).then_inc(y_done, 1)
                    dve.wait_ge(y_done, t + 1)
                    V.tensor_tensor(yb[:], y[:], b2_sb[:], ALU.add).then_inc(yb_done, 1)
                if s == 1 and (not isinstance(t, int) or t > 0):
                    last_norm(t - 1)
                if s == 3:
                    dve.wait_ge(o_mm, t + 1)
                    dve.wait_ge(yb_done, t + 1)
                    at_least(dve, o_done, t)
                    V.tensor_tensor(z[:], o_ps[0:NT, 0:D], yb[:], ALU.add).then_inc(z_done, 1)
                    dve.wait_ge(z_done, t + 1)
                    V.bn_stats(st2[:], z[:]).then_inc(stats2, 1)
                    dve.wait_ge(stats2, t + 1)
                    V.memset(carrier[:], 0.0)
                    V.bn_aggr(mv2[:], st2[:]).then_inc(var2, 1)

            def wide_window(n, w, k):
                p, g = shape_of(n)
                at_least(dve, wide_mm, k)
                at_least(dve, base_moved, k + n + 1)
                V.tensor_tensor(oh_wide[0:p, 0:g, :], dst_w[0:p, 0:g].unsqueeze(2).to_broadcast([p, g, WIDE]),
                                iota_win[0:p, :].unsqueeze(1).to_broadcast([p, g, WIDE]),
                                ALU.is_equal).then_inc(wide_oh, 1)
                dve.wait_ge(wide_oh, k + 1)
                V.tensor_scalar(dst_w[0:p, 0:g], dst_w[0:p, 0:g], float(-WIDE), None, ALU.add).then_inc(base_moved, 1)
                dve.wait_ge(wide_mm, k + 1)
                at_least(dve, wide_add, k)
                for c in range(KC):
                    to = aggT[:, c, bass.ds(w * WIDE, WIDE)]
                    last = V.tensor_tensor(to, to, agg_ps[c][:, :], ALU.add)
                last.then_inc(wide_add, 1)

            def general_group(n):
                p, g = shape_of(n)
                k0 = n * WINDOWS
                at_least(dve, base_moved, n * (WINDOWS + 1))
                V.tensor_copy(dst_w[0:p, 0:g], dst_f[0:p, n, 0:g]).then_inc(base_moved, 1)
                wide_window(n, 0, k0)
                with dve.Fori(1, WINDOWS) as w:
                    wide_window(n, w, k0 + w)

            by_flag(dve, fast, lambda: general_pass(dve, general_group, dense, nothing, last_norm))

        @block.tensor
        def _(pe):
            T = nc.tensor
            pe.wait_ge(pool_consts, 8)
            pe.wait_ge(consts, 3)
            for a in range(2):
                pe.wait_ge(converted[a], 1)
                for c in range(4):
                    for g in range(G):
                        last = T.transpose(bank[4 * a + c][:, g * CH:(g + 1) * CH],
                                           raw_f[:, 4 * a + c, :].rearrange("n (p g) -> n g p", g=G)[:, g, :],
                                           ident[0:CH, 0:CH])
                    last.then_inc(idx_turned[a], 1)
            pe.wait_ge(based, 1)
            T.matmul(setup_ps[:, 0:NG], ones[0:1, :], base_f[:], start=True, stop=True).then_inc(base_bc, 1)
            pe.wait_ge(check_step, 7)
            T.transpose(setup_ps[0:1, 0:P], worst[:, 2:3], ident[:]).then_inc(worst_T, 1)

            def spread(n, i, s):
                p, g = shape_of(n)
                pe.wait_ge(src_copied, n + 1)
                at_least(pe, same_done, n - 1)
                for k in range(g):
                    for part in range(2):
                        last = T.matmul(src_ps[s % 2][0:p, k * P:k * P + p],
                                        srcs[0:p, s, part, k:k + 1].to_broadcast([p, p]), ident_b[0:p, 0:p],
                                        start=part == 0, stop=part == 1)
                last.then_inc(src_spread, 1)

            def add_same(n, i, s):
                p, g = shape_of(n)
                b = s % 2
                pe.wait_ge(same_done, n + 1)
                pe.wait_ge(attr_in[s], 16 * (i + 1))
                at_least(pe, staged, n - 1)
                at_least(pe, idx_done, n - 1)
                for k in range(g):
                    T.matmul(sum_ps[b][0:p, k * ROW:k * ROW + DE], same[0:p, b, k, 0:p], attr[0:p, s, k, :],
                             start=True, stop=True)
                pe.wait_ge(earlier_done, n + 1)
                for k in range(g):
                    T.matmul(sum_ps[b][0:p, k * ROW + DE:(k + 1) * ROW], earlier[0:p, b, k, 0:p], ones_b[0:p, :],
                             start=True, stop=True)
                    last = T.matmul(rep_ps[b][0:p, k:k + 1], earlier[0:p, b, k, 0:p], ones_b[0:p, :],
                                    start=True, stop=True)
                last.then_inc(summed, 1)

            def deg_count(m, b, first, final):
                pe.wait_ge(deg_oh, m + 1)
                for g in range(G):
                    last = T.matmul(deg_ps[0:HI, 0:P], oh_hi[:, b, :].rearrange("p (v g) -> p g v", g=G)[:, g, :],
                                    oh_lo[:, b, :].rearrange("p (v g) -> p g v", g=G)[:, g, :],
                                    start=first and g == 0, stop=final and g == G - 1)
                last.then_inc(deg_mm, 1)

            def edge_step(n, i, s, kind):
                spread(n, i, s)
                if kind == "deg" and (not isinstance(n, int) or n > 0):
                    deg_count(2 * n - 2, 0, isinstance(n, int) and n == 1, False)
                    deg_count(2 * n - 1, 1, False, False)
                if not isinstance(n, int) or n > 0:
                    add_same(n - 1, i if s > 0 else i - 1, (s - 1) % 4)

            def turn_dis():
                deg_count(NG - 2, 0, False, False)
                deg_count(NG - 1, 1, False, True)
                pe.wait_ge(dis_loaded, 16)
                T.transpose(setup_ps[0:NT, 256:256 + TILES], dis_t[:], ident[0:TILES, 0:TILES]).then_inc(dis_turned, 1)

            edge_pass(pe, edge_step, turn_dis, nothing, lambda: add_same(NG - 1, ITER - 1, (NG - 1) % 4))

            pe.wait_ge(weights_in, 16 * 8)
            for j in range(HC):
                last = T.matmul(setup_ps[:, 400 + j:401 + j], W1u_sb[:, j * P:(j + 1) * P], u_sb[:], start=True, stop=True)
            last.then_inc(bias_mm, 1)
            pe.wait_ge(staged, NG)
            pe.wait_ge(idx_done, NG)
            pe.wait_ge(bias_done, 1)

            def sum_window(n, i, s):
                p, g = shape_of(n)
                b = s % 2
                pe.wait_ge(gathered[s], 16 * (G * i + g))
                pe.wait_ge(oh_ready, n + 1)
                at_least(pe, agg_added, n - 1)
                for c in range(KC):
                    for k in range(g):
                        for part in range(PARTS):
                            at = part * D + c * P
                            last = T.matmul(agg_ps[b][:, c * WIN:(c + 1) * WIN], rows[0:p, s, k, at:at + P],
                                            oh[0:p, b, k, :], start=k == 0 and part == 0,
                                            stop=k == g - 1 and part == PARTS - 1)
                last.then_inc(agg_mm, 1)

            def dense(t, s, adds):
                if s == 0:
                    pe.wait_ge(aggw_ready, t + 1)
                    at_least(pe, r_done, t)
                    for c in range(KC):
                        last = T.matmul(l0_ps[0:NT, 0:D], aggw[:, c, :], W_sb[:, c, :], start=c == 0, stop=c == KC - 1)
                    last.then_inc(l0_mm, 1)
                if s == 1:
                    pe.wait_ge(y_done, t + 1)
                    pe.wait_ge(emean_done, t + 1)
                    at_least(pe, turned_out, 2 * t)
                    for c in range(KC):
                        T.transpose(tr_ps[:, c * NT:(c + 1) * NT], y[:, c * P:(c + 1) * P], ident[0:NT, 0:NT])
                    T.transpose(tr_ps[0:DE, KC * NT:(KC + 1) * NT], emean[:], ident[0:NT, 0:NT]).then_inc(turned, 1)
                if s == 2:
                    pe.wait_ge(turned_out, 2 * (t + 1))
                    at_least(pe, h_relu, t)
                    for j in range(HC):
                        for c in range(KC):
                            T.matmul(h_ps[:, j * NT:(j + 1) * NT], W1_sb[:, c, j * P:(j + 1) * P], yT[:, c, :],
                                     start=c == 0, stop=False)
                        last = T.matmul(h_ps[:, j * NT:(j + 1) * NT], W1e_sb[:, j * P:(j + 1) * P], eT[:],
                                        start=False, stop=True)
                    last.then_inc(h_mm, 1)
                if s == 3:
                    pe.wait_ge(h_relu, t + 1)
                    at_least(pe, z_done, t)
                    for j in range(HC):
                        last = T.matmul(o_ps[0:NT, 0:D], hT[:, j, :], W2_sb[:, j, :], start=j == 0, stop=j == HC - 1)
                    last.then_inc(o_mm, 1)

            def wide_window(n, k):
                p, g = shape_of(n)
                pe.wait_ge(wide_oh, k + 1)
                at_least(pe, wide_add, k)
                for c in range(KC):
                    for j in range(g):
                        for part in range(PARTS):
                            at = part * D + c * P
                            last = T.matmul(agg_ps[c][:, :], rows[0:p, 0, j, at:at + P], oh_wide[0:p, j, :],
                                            start=j == 0 and part == 0, stop=j == g - 1 and part == PARTS - 1)
                last.then_inc(wide_mm, 1)

            def general_group(n):
                pe.wait_ge(gathered[0], 16 * G * (n + 1) if shape_of(n)[1] == G else 16 * (G * n + 1))
                wide_window(n, n * WINDOWS)
                with pe.Fori(1, WINDOWS) as w:
                    wide_window(n, n * WINDOWS + w)

            by_flag(pe,
                    lambda: node_pass(pe, sum_window, dense, nothing),
                    lambda: general_pass(pe, general_group, dense))


_INS = ['x', 'src', 'dst', 'edge_attr_64', 'L0_gnn_W', 'L1_gnn_u', 'L1_gnn_W1', 'L1_gnn_b1', 'L1_gnn_W2', 'L1_gnn_b2']


def kernel(**inputs):
    import numpy as _np
    import concourse.bacc as _bacc
    from concourse import mybir as _mybir
    from concourse.bass_utils import run_bass_kernel_spmd as _run

    nc = _bacc.Bacc("TRN2", target_bir_lowering=False, num_devices=1)
    arrays, args = {}, []
    for name in _INS:
        a = _np.ascontiguousarray(inputs[name])
        arrays[f"in_{name}_dram"] = a
        args.append(nc.dram_tensor(f"in_{name}_dram", a.shape, _mybir.dt.from_np(a.dtype), kind="ExternalInput").ap())
    out = nc.dram_tensor("out_0_dram", inputs['x'].shape, _mybir.dt.float32, kind="ExternalOutput").ap()
    gnn_kernel(nc, *args, out)
    r = _run(nc, [arrays], core_ids=[0])
    return r.results[0]["out_0_dram"]
```
